# Optimizing a Trainium2 kernel written in Bass

```python
import numpy as np
import jax
import jax.numpy as jnp

def _softmax(x, axis=-1):
    return jax.nn.softmax(x, axis=axis)

def _gelu(x):
    return jax.nn.gelu(x, approximate=True)

def _silu(x):
    return jax.nn.silu(x)

def _sigmoid(x):
    return jax.nn.sigmoid(x)

def _layernorm(x, axis=-1, eps=1e-05):
    m = jnp.mean(x, axis=axis, keepdims=True)
    v = jnp.var(x, axis=axis, keepdims=True)
    return (x - m) / jnp.sqrt(v + eps)

def _scatter_add(tgt, idx, src, axis=0):
    return tgt.at[idx].add(src)

def _segment_sum(src, seg, n):
    return jax.ops.segment_sum(src, seg, n)
kernel_name = 'mk_xattn_ffn_d1_seqx_r4_693b3c'

def setup_inputs(seed: int=0):
    np.random.seed(seed)
    _w = jnp.asarray

    def _rec_inputs():
        import jax
        import jax.numpy as jnp
        _rk = jax.random.key(seed)
        x = -0.0002928 + 1 * jax.random.normal(jax.random.fold_in(_rk, 1), (8, 512, 256), jnp.float32)
        _lenS = 512 - jax.random.randint(jax.random.fold_in(_rk, 7), (8,), 0, max(1, 512 // 4) + 1, jnp.int32)
        _lenS2 = 512 - jax.random.randint(jax.random.fold_in(_rk, 8), (8,), 0, max(1, 512 // 4) + 1, jnp.int32)
        _ctx_1024P = jax.random.normal(jax.random.fold_in(_rk, 11), (8, 16, 256), jnp.float32)
        _ctx_1024c = jax.random.dirichlet(jax.random.fold_in(_rk, 511), 0.3 * jnp.ones((16,), jnp.float32), (8, 512))
        _ctx_1024t = jnp.einsum('bsk,bkd->bsd', _ctx_1024c, _ctx_1024P)
        _ctx_1024t = _ctx_1024t * jax.lax.rsqrt(jnp.mean(jnp.square(_ctx_1024t)) + 1e-12) * 0.953939
        ctx_1024 = 0.000227908 + 0.99994 * (_ctx_1024t + 0.3 * jax.random.normal(jax.random.fold_in(_rk, 611), (8, 512, 256), jnp.float32))
        return (x, ctx_1024)
    x, ctx_1024 = _rec_inputs()

    def _L0_xattn_setup():
        import jax, jax.numpy as jnp
        import numpy as np
        HEADS = 16
        key = jax.random.key(seed)
        ks = jax.random.split(key, 6)
        b, n, m, dim = (2, 512, 128, 256)
        s = dim ** (-0.5)
        return {'x': jax.random.normal(ks[0], (b, n, dim), jnp.float32), 'mem': jax.random.normal(ks[1], (b, m, dim), jnp.float32), 'Wq': jax.random.normal(ks[2], (dim, dim), jnp.float32) * s, 'Wkv': jax.random.normal(ks[3], (dim, 2 * dim), jnp.float32) * s, 'Wout': jax.random.normal(ks[4], (dim, dim), jnp.float32) * s, 'bout': jnp.zeros((dim,), jnp.float32)}
    _L0_xattn_all = _L0_xattn_setup()
    _L0_xattn_in = {k: v for k, v in _L0_xattn_all.items() if k in ('Wq', 'Wkv', 'Wout', 'bout')}
    del _L0_xattn_all

    def _L0_ffn_setup():
        import jax, jax.numpy as jnp
        import numpy as np
        LATENT = 256
        LEAF_W = 64
        DEPTH = 4
        N_LEAVES = 2 ** DEPTH
        N_NODES = 2 ** DEPTH - 1
        B, S = (4, 512)

        def _fff_params(key, prefix):
            ks = jax.random.split(key, 4)
            d, h, l, n = (LATENT, LEAF_W, N_LEAVES, N_NODES)
            s_in = 1.0 / np.sqrt(d).astype(np.float32)
            s_h = 1.0 / np.sqrt(h).astype(np.float32)
            return {f'{prefix}_node_w': jax.random.normal(ks[0], (n, d), jnp.float32) * s_in, f'{prefix}_node_b': jax.random.normal(ks[1], (n,), jnp.float32) * s_in, f'{prefix}_w1': jax.random.normal(ks[2], (l, d, h), jnp.float32) * s_in, f'{prefix}_b1': jnp.zeros((l, h), jnp.float32), f'{prefix}_w2': jax.random.normal(ks[3], (l, h, d), jnp.float32) * s_h, f'{prefix}_b2': jnp.zeros((l, d), jnp.float32)}

        def _fff(x, node_w, node_b, w1, b1, w2, b2):
            Bx, Sx, D = x.shape
            xf = x.reshape(-1, D)
            N = xf.shape[0]
            cur = jnp.zeros((N,), jnp.int32)
            for _ in range(DEPTH):
                pw = node_w[cur]
                score = jnp.einsum('nd,nd->n', xf, pw) + node_b[cur]
                cur = 2 * cur + 1 + (score >= 0).astype(jnp.int32)
            leaf = cur - N_NODES
            sel = jax.nn.one_hot(leaf, N_LEAVES, dtype=xf.dtype)
            hidden_all = jax.nn.relu(jnp.einsum('nd,ldh->lnh', xf, w1) + b1[:, None, :])
            hidden = hidden_all * sel.T[:, :, None]
            out = jnp.einsum('lnh,lho->no', hidden, w2) + sel @ b2
            return out.reshape(Bx, Sx, D)
        key = jax.random.key(seed)
        kx, kq, kk, kv = jax.random.split(key, 4)
        inp = {'x': jax.random.normal(kx, (B, S, LATENT), jnp.float32)}
        inp.update(_fff_params(kq, 'q'))
        inp.update(_fff_params(kk, 'k'))
        inp.update(_fff_params(kv, 'v'))
        return inp
    _L0_ffn_all = _L0_ffn_setup()
    _L0_ffn_in = {k: v for k, v in _L0_ffn_all.items() if k in ('q_node_w', 'q_node_b', 'q_w1', 'q_b1', 'q_w2', 'q_b2', 'k_node_w', 'k_node_b', 'k_w1', 'k_b1', 'k_w2', 'k_b2', 'v_node_w', 'v_node_b', 'v_w1', 'v_b1', 'v_w2', 'v_b2')}
    del _L0_ffn_all
    return {'x': x, 'ctx_1024': ctx_1024, 'L0_xattn_Wq': _L0_xattn_in['Wq'], 'L0_xattn_Wkv': _L0_xattn_in['Wkv'], 'L0_xattn_Wout': _L0_xattn_in['Wout'], 'L0_xattn_bout': _L0_xattn_in['bout'], 'L0_ffn_q_node_w': _L0_ffn_in['q_node_w'], 'L0_ffn_q_node_b': _L0_ffn_in['q_node_b'], 'L0_ffn_q_w1': _L0_ffn_in['q_w1'], 'L0_ffn_q_b1': _L0_ffn_in['q_b1'], 'L0_ffn_q_w2': _L0_ffn_in['q_w2'], 'L0_ffn_q_b2': _L0_ffn_in['q_b2'], 'L0_ffn_k_node_w': _L0_ffn_in['k_node_w'], 'L0_ffn_k_node_b': _L0_ffn_in['k_node_b'], 'L0_ffn_k_w1': _L0_ffn_in['k_w1'], 'L0_ffn_k_b1': _L0_ffn_in['k_b1'], 'L0_ffn_k_w2': _L0_ffn_in['k_w2'], 'L0_ffn_k_b2': _L0_ffn_in['k_b2'], 'L0_ffn_v_node_w': _L0_ffn_in['v_node_w'], 'L0_ffn_v_node_b': _L0_ffn_in['v_node_b'], 'L0_ffn_v_w1': _L0_ffn_in['v_w1'], 'L0_ffn_v_b1': _L0_ffn_in['v_b1'], 'L0_ffn_v_w2': _L0_ffn_in['v_w2'], 'L0_ffn_v_b2': _L0_ffn_in['v_b2']}

def reference(x, ctx_1024, L0_xattn_Wq, L0_xattn_Wkv, L0_xattn_Wout, L0_xattn_bout, L0_ffn_q_node_w, L0_ffn_q_node_b, L0_ffn_q_w1, L0_ffn_q_b1, L0_ffn_q_w2, L0_ffn_q_b2, L0_ffn_k_node_w, L0_ffn_k_node_b, L0_ffn_k_w1, L0_ffn_k_b1, L0_ffn_k_w2, L0_ffn_k_b2, L0_ffn_v_node_w, L0_ffn_v_node_b, L0_ffn_v_w1, L0_ffn_v_b1, L0_ffn_v_w2, L0_ffn_v_b2):
    import jax
    import jax.numpy as jnp

    def _L0_xattn_ref(x, mem, Wq, Wkv, Wout, bout):
        import jax, jax.numpy as jnp
        import numpy as np
        HEADS = 16
        b, n, dim = x.shape
        h = HEADS
        d = dim // h
        scale = d ** (-0.5)
        mem_len = mem.shape[1]
        q = x @ Wq
        xc = jnp.concatenate((mem, x), axis=1)
        kv = xc @ Wkv
        k, v = jnp.split(kv, 2, axis=-1)

        def to_heads(t):
            bb, nn, _ = t.shape
            return t.reshape(bb, nn, h, d).transpose(0, 2, 1, 3)
        q, k, v = (to_heads(q), to_heads(k), to_heads(v))
        dots = jnp.einsum('bhid,bhjd->bhij', q, k) * scale
        j = dots.shape[-1]
        i_idx = jnp.arange(n)[:, None]
        j_idx = jnp.arange(j)[None, :]
        mask = j_idx > i_idx + mem_len
        dots = jnp.where(mask[None, None], -jnp.inf, dots)
        attn = jax.nn.softmax(dots, axis=-1)
        out = jnp.einsum('bhij,bhjd->bhid', attn, v)
        out = out.transpose(0, 2, 1, 3).reshape(b, n, dim)
        return out @ Wout + bout

    def _L0_ffn_ref(x, q_node_w, q_node_b, q_w1, q_b1, q_w2, q_b2, k_node_w, k_node_b, k_w1, k_b1, k_w2, k_b2, v_node_w, v_node_b, v_w1, v_b1, v_w2, v_b2):
        import jax, jax.numpy as jnp
        import numpy as np
        LATENT = 256
        LEAF_W = 64
        DEPTH = 4
        N_LEAVES = 2 ** DEPTH
        N_NODES = 2 ** DEPTH - 1
        B, S = (4, 512)

        def _fff_params(key, prefix):
            ks = jax.random.split(key, 4)
            d, h, l, n = (LATENT, LEAF_W, N_LEAVES, N_NODES)
            s_in = 1.0 / np.sqrt(d).astype(np.float32)
            s_h = 1.0 / np.sqrt(h).astype(np.float32)
            return {f'{prefix}_node_w': jax.random.normal(ks[0], (n, d), jnp.float32) * s_in, f'{prefix}_node_b': jax.random.normal(ks[1], (n,), jnp.float32) * s_in, f'{prefix}_w1': jax.random.normal(ks[2], (l, d, h), jnp.float32) * s_in, f'{prefix}_b1': jnp.zeros((l, h), jnp.float32), f'{prefix}_w2': jax.random.normal(ks[3], (l, h, d), jnp.float32) * s_h, f'{prefix}_b2': jnp.zeros((l, d), jnp.float32)}

        def _fff(x, node_w, node_b, w1, b1, w2, b2):
            Bx, Sx, D = x.shape
            xf = x.reshape(-1, D)
            N = xf.shape[0]
            cur = jnp.zeros((N,), jnp.int32)
            for _ in range(DEPTH):
                pw = node_w[cur]
                score = jnp.einsum('nd,nd->n', xf, pw) + node_b[cur]
                cur = 2 * cur + 1 + (score >= 0).astype(jnp.int32)
            leaf = cur - N_NODES
            sel = jax.nn.one_hot(leaf, N_LEAVES, dtype=xf.dtype)
            hidden_all = jax.nn.relu(jnp.einsum('nd,ldh->lnh', xf, w1) + b1[:, None, :])
            hidden = hidden_all * sel.T[:, :, None]
            out = jnp.einsum('lnh,lho->no', hidden, w2) + sel @ b2
            return out.reshape(Bx, Sx, D)
        q = _fff(x, q_node_w, q_node_b, q_w1, q_b1, q_w2, q_b2)
        k = _fff(x, k_node_w, k_node_b, k_w1, k_b1, k_w2, k_b2)
        v = _fff(x, v_node_w, v_node_b, v_w1, v_b1, v_w2, v_b2)
        scale = 1.0 / np.sqrt(LATENT).astype(np.float32)
        attn = jax.nn.softmax(jnp.einsum('bqd,bkd->bqk', q, k) * scale, axis=-1)
        return jnp.einsum('bqk,bkd->bqd', attn, v)
    x = x + _L0_xattn_ref(_layernorm(x, axis=-1), ctx_1024, L0_xattn_Wq, L0_xattn_Wkv, L0_xattn_Wout, L0_xattn_bout)
    x = x + _L0_ffn_ref(_layernorm(x, axis=-1), L0_ffn_q_node_w, L0_ffn_q_node_b, L0_ffn_q_w1, L0_ffn_q_b1, L0_ffn_q_w2, L0_ffn_q_b2, L0_ffn_k_node_w, L0_ffn_k_node_b, L0_ffn_k_w1, L0_ffn_k_b1, L0_ffn_k_w2, L0_ffn_k_b2, L0_ffn_v_node_w, L0_ffn_v_node_b, L0_ffn_v_w1, L0_ffn_v_b1, L0_ffn_v_w2, L0_ffn_v_b2)
    return x

_drawn_inputs = setup_inputs


def setup_inputs(seed=0):
    import zlib

    import numpy as np

    out = dict(_drawn_inputs(seed))
    spreads = {'L0_xattn_bout': (0.0, 0.1),
     'L0_ffn_q_b1': (0.0, 0.8),
     'L0_ffn_q_b2': (0.0, 0.8),
     'L0_ffn_k_b1': (0.0, 0.8),
     'L0_ffn_k_b2': (0.0, 0.8),
     'L0_ffn_v_b1': (0.0, 0.577),
     'L0_ffn_v_b2': (0.0, 0.304)}
    factors = {'L0_ffn_q_node_w': 3.646,
     'L0_ffn_q_node_b': 8.0,
     'L0_ffn_q_w1': 4.258,
     'L0_ffn_q_w2': 3.536,
     'L0_ffn_k_node_w': 3.593,
     'L0_ffn_k_node_b': 8.0,
     'L0_ffn_k_w1': 4.167,
     'L0_ffn_k_w2': 3.576,
     'L0_ffn_v_node_b': 3.066}
    for name, (base, spread) in spreads.items():
        noise = np.random.default_rng([zlib.crc32(name.encode()), seed]).standard_normal(out[name].shape)
        drawn = base * np.exp(spread * noise) if base else spread * noise
        out[name] = jnp.asarray(drawn.astype(out[name].dtype))
    for name, factor in factors.items():
        out[name] = (out[name] * factor).astype(out[name].dtype)
    return out
```

```python
from contextlib import ExitStack

import concourse.bass as bass
from concourse import mybir

F32 = mybir.dt.float32
BF16 = mybir.dt.bfloat16
ALU = mybir.AluOpType
ACT = mybir.ActivationFunctionType
AX = mybir.AxisListType

P = 128
B, N, D = 8, 512, 256
H = 16
DH = D // H
HG = 4
G = H // HG
T = N // P
KC = D // P
J = 2 * N
JT = J // P
LEAVES, LEAF_W, NODES = 16, 64, 15
BR = 3
HID = LEAVES * LEAF_W
HT = HID // P
PARTS = 3
PAIRS = ((0, 0), (0, 1), (1, 0), (1, 1), (0, 2), (2, 0))
SK = len(PAIRS) * DH
VW = DH + 1
BIG = 1e30
EPS = 1e-5
SCALE1 = float(DH) ** -0.5
SCALE2 = float(D) ** -0.5

UNITS = G * JT
STILES = H * T
LEAD = 22
RQ = 2 * len(PAIRS)
STACK_DMAS = RQ + 2 * len(PAIRS)

FRONT_D = [("q",), ("k", 0), ("k", 1), ("v", 0), ("v", 1)]
M_AT = 5
FRONT_A = [("xT", 0), ("xT", 1), ("cT", 0), ("cT", 1)]


def lead_tiles(where):
    if where in (1, 2):
        return [HT * (where - 1) + n for n in range(HT)]
    t = where[1]
    rest = list(range(2 * HT, LEAD))
    return rest[:2] if t == 0 else rest[t + 1:t + 2] if t < T else rest[T + 1:]


def batch_d(more):
    keys = []
    for u in range(UNITS):
        keys += [("s", n) for n in (LEAD + 2 * u, LEAD + 2 * u + 1) if n < STILES]
        if u % JT == 1 and u > JT:
            keys += [("oT", u // JT - 1)]
    keys += [("oT", G - 1)] + (FRONT_D[:1] if more else []) + [("out", 0), ("out", 1)]
    keys += FRONT_D[1:] if more else []
    keys += [("node",)]
    for r in range(BR):
        keys += [("s", n) for n in lead_tiles(r)] if more and r > 0 else []
        keys += [("f", r)] if r < 2 else [("f", 2), ("f", 3)]
    for t in range(T + 1):
        keys += [("s", n) for n in lead_tiles(("pT", t))] if more else []
        keys += [("pT", t)] if t < T else []
    return keys + [("y", 0), ("y", 1)]


def batch_a(more):
    keys = [("e", 0, h) for h in range(HG)]
    for u in range(UNITS):
        if u < UNITS - 1:
            keys += [("e", u + 1, h) for h in range(HG)]
        if u % JT == M_AT and u // JT < G - 1:
            keys += [("m", u // JT + 1)]
    keys += FRONT_A if more else []
    keys += [("dT", 0), ("dT", 1)]
    keys += [("yT", 0), ("yT", 1), ("one", 0), ("one", 1), ("one", 2)]
    keys += [("h", r, t) for r in range(BR) for t in range(HT)]
    keys += [("x", t) for t in range(T)]
    return keys + ([("m", 0)] if more else [])


class Ring:

    def __init__(self, slots, before, batch, last):
        assert len(batch) % slots == 0, len(batch)
        self.slots, self.per, first = slots, len(batch), len(before)
        self.number = {
            "before": {key: n for n, key in enumerate(before)},
            "batch": {key: first + n for n, key in enumerate(batch)},
            "last": {key: first + n for n, key in enumerate(last)},
        }

    def slot(self, at, key):
        return self.number[at[0]][key] % self.slots

    def count(self, at, key):
        return at[1] * self.per + self.number[at[0]][key] + 1

    def wait_free(self, engine, at, key, emptied):
        if self.number[at[0]][key] >= self.slots:
            engine.wait_ge(emptied, self.count(at, key) - self.slots)


def chain_keys(where):
    mx = {n: ("mx", n // (HG * T)) for n in range(HG * T - 1, STILES, HG * T)}
    lead = [mx[n] for n in range(LEAD) if n in mx]
    front = [("part", s) for s in range(3)]
    if where == "before":
        return [("ln1", 0), ("ln1", 1)] + [(b, n) for b in ("b2", "b1") for n in range(4)
                                           if (b, n) != ("b1", 3)] + front + lead
    more = where == "batch"
    keys = []
    for u in range(UNITS):
        keys += [mx[n] for n in (LEAD + 2 * u, LEAD + 2 * u + 1) if n in mx]
        if u % JT == 1 and u > JT:
            keys += [("oT", u // JT - 1)]
        if more and u == 12:
            keys += [("ln1", 0), ("ln1", 1)]
    keys += [("oT", G - 1)] + (front[:1] if more else []) + [("ln2", 0), ("ln2", 1)]
    keys += front[1:] + [mx[n] for n in range(2 * HT) if n in mx] if more else []
    keys += [("x", t) for t in range(T)]
    keys += [mx[n] for n in range(2 * HT, LEAD) if n in mx] if more else []
    return keys + [("sum",)]


CHAIN_BATCH = chain_keys("batch")
CHAIN = {"before": {key: n for n, key in enumerate(chain_keys("before"))}}
CHAIN |= {w: {key: n + len(CHAIN["before"]) for n, key in enumerate(chain_keys(w))}
          for w in ("batch", "last")}
RING_D = Ring(2, FRONT_D + [("s", n) for n in range(LEAD)], batch_d(True), batch_d(False))
RING_A = Ring(3, FRONT_A + [("m", 0)], batch_a(True), batch_a(False))


def program(nc, x, ctx, wq, wkv, wout, bout, ffn, c_ident, c_mask, c_path, c_flip, out):
    es = ExitStack()
    with es:
        def sb(name, shape, dt=F32):
            return es.enter_context(nc.sbuf_tensor(name, shape, dt))

        def sem(name):
            return es.enter_context(nc.semaphore(name))

        x_in = sb("x_in", [P, T, D])
        ctx_in = sb("ctx_in", [P, T, D])
        xn = sb("xn", [P, T, D])
        res = sb("res", [P, T, D])
        xnT = sb("xnT", [P, KC, N])
        cT = sb("cT", [P, KC, N])
        yT = sb("yT", [P, KC, N])
        oT = yT
        o_sb = sb("o_sb", [P, T, D])
        y_sb = o_sb
        pv_sb = sb("pv_sb", [P, N])
        parts = sb("parts", [P, PARTS, 3, J], BF16)
        p2 = parts[:, :, :, :].rearrange("p a b c -> p (a b c)").bitcast(F32)[:, 0:T * N].rearrange(
            "p (t n) -> p t n", t=T)
        qs = sb("qs", [P, H, N], BF16)
        ks = sb("ks", [P, H, J], BF16)
        v_sb = sb("v_sb", [P, JT, H, VW])
        shared = sb("shared", [P, 3 * HG * N])
        probs = shared[:, :].rearrange("p (s h n) -> p s h n", s=3, h=HG)
        hidden = shared[:, 0:HT * N].rearrange("p (t n) -> p t n", t=HT)
        qk2T = shared[:, HT * N:HT * N + 2 * KC * N].rearrange("p (r k n) -> p r k n", r=2, k=KC)
        p2T = shared[:, 0:T * N].rearrange("p (t n) -> p t n", t=T)
        rest = shared[:, 4608:4608 + J]
        g0 = shared[0:96, 4096:4096 + N // 2].bitcast(BF16)
        v2 = sb("v2", [P, T, D])
        wq_sb = sb("wq_sb", [P, KC, D])
        wkv_sb = sb("wkv_sb", [P, KC, 2 * D])
        wout_sb = sb("wout_sb", [P, KC, D])
        w1 = sb("w1", [P, BR, KC, HID])
        w2 = sb("w2", [P, BR, HT, D])
        mk = sb("mk", [P, BR * HT, P], BF16)
        ohm = sb("ohm", [P, BR, 48], BF16)
        b2s = sb("b2s", [48, BR, D], BF16)
        node = sb("node", [P, KC, 96])
        identf = sb("identf", [P, P])
        identb = sb("identb", [P, P], BF16)
        maskb = sb("maskb", [P, P], BF16)
        bias = sb("bias", [P, D])
        path = sb("path", [96, BR * LEAVES])
        flip = sb("flip", [96, 1])
        nb = sb("nb", [96, 1])
        gates = sb("gates", [P, N], BF16)
        onehot = cT[0:48, :, :].rearrange("p k n -> p (k n)")[:, 0:BR * N // 2].bitcast(BF16).rearrange(
            "p (r n) -> p r n", r=BR)
        rowmax = sb("rowmax", [P, G, T, HG])
        mx2 = sb("mx2", [P, G, T, 2, HG], BF16)
        mrow = sb("mrow", [2 * HG, N], BF16)
        st = sb("st", [P, T, 6])
        mv = sb("mv", [P, T, 2])
        ve = sb("ve", [P, T])
        rstd = sb("rstd", [P, T])
        st2 = sb("st2", [P, T, 6])
        mv2 = sb("mv2", [P, T, 2])
        ve2 = sb("ve2", [P, T])
        rstd2 = sb("rstd2", [P, T])
        half = sb("half", [P, T])
        carrier_p, carrier_v = sb("carrier_p", [P, UNITS]), sb("carrier_v", [P, 1])
        rinv = sb("rinv", [P, G, T, HG])
        nmax = sb("nmax", [P, T])
        nmaxs = sb("nmaxs", [P, T])
        sums = sb("sums", [P, T])
        rs2 = sb("rs2", [P, T])
        b2raw = shared[0:48, 0:BR * D].rearrange("p (r d) -> p r d", r=BR)
        b2rem = shared[0:48, BR * D:2 * BR * D].rearrange("p (r d) -> p r d", r=BR)
        b2p = [shared[0:48, (4 + k) * 512:(5 + k) * 512].bitcast(BF16)[:, 0:BR * D].rearrange(
            "p (r d) -> p r d", r=BR) for k in range(PARTS)]
        b1raw = shared[0:BR * HT, 3584:3584 + P]
        b1rem = shared[0:BR * HT, 3712:3712 + P]
        b1p = [shared[0:BR * HT, 3840 + 64 * k:3904 + 64 * k].bitcast(BF16) for k in range(PARTS)]
        noderaw = shared[0:96, 4096:4096 + D]
        maskf = shared[:, 4352:4352 + P]

        ps_d = es.enter_context(nc.psum_tensor("ps_d", [P, 2, 1024], F32))
        ps_a = es.enter_context(nc.psum_tensor("ps_a", [P, 3, 512], F32))
        ps_o = es.enter_context(nc.psum_tensor("ps_o", [P, 512], F32))

        d_full, d_done = sem("d_full"), sem("d_done")
        a_full, a_done = sem("a_full"), sem("a_done")
        x_loaded, ctx_loaded = sem("x_loaded"), sem("ctx_loaded")
        wqkv_loaded, const_loaded = sem("wqkv_loaded"), sem("const_loaded")
        ffn_loaded, raw_loaded = sem("ffn_loaded"), sem("raw_loaded")
        raw_zeroed, pool_setup, dve_setup = sem("raw_zeroed"), sem("pool_setup"), sem("dve_setup")
        bias_split, bias_rows = sem("bias_split"), sem("bias_rows")
        node_turned, node_done = sem("node_turned"), sem("node_done")
        var1, rstd1_done, var2, rstd2_done = sem("var1"), sem("rstd1_done"), sem("var2"), sem("rstd2_done")
        xn_done, yn_done, res_done = sem("xn_done"), sem("yn_done"), sem("res_done")
        part1_done, parts_done, stacked = sem("part1_done"), sem("parts_done"), sem("stacked")
        max_split, mrow_stacked = sem("max_split"), sem("mrow_stacked")
        masked, pv_done, pv_copied = sem("masked"), sem("pv_done"), sem("pv_copied")
        gates_done, max2_done, stored = sem("gates_done"), sem("max2_done"), sem("stored")
        chain = sem("chain")
        block = es.enter_context(nc.Block())

        def first_column(jt):
            return 0 if jt < T else P * (jt - T)

        def rows_of(array, b):
            return array[bass.ds(b, 1)].rearrange("o (t p) d -> p (o t) d", p=P)

        def d_slot(at, key):
            return ps_d[:, RING_D.slot(at, key), :]

        def a_slot(at, key):
            return ps_a[:, RING_A.slot(at, key), :]

        @block.sync
        def _(sp):
            def load(dst, src, signal):
                sp.dma_start(dst, src).then_inc(signal, 16)

            load(x_in[:, :, :], rows_of(x, 0), x_loaded)
            load(ctx_in[:, :, :], rows_of(ctx, 0), ctx_loaded)
            load(identf[:, :], c_ident, const_loaded)
            load(wq_sb[:, :, :], wq.rearrange("(k p) n -> p k n", p=P), wqkv_loaded)
            load(wkv_sb[:, :, :], wkv.rearrange("(k p) n -> p k n", p=P), wqkv_loaded)
            load(maskf, c_mask, const_loaded)
            load(path[:, :], c_path, const_loaded)
            load(flip[:, :], c_flip, const_loaded)
            load(bias[:, :], bout.partition_broadcast(P), const_loaded)
            load(wout_sb[:, :, :], wout.rearrange("(k p) n -> p k n", p=P), const_loaded)
            sp.wait_ge(raw_zeroed, 2)
            for r in range(BR):
                node_w, node_b, w1_d, b1_d, w2_d, b2_d = ffn[r]
                for copy in range(2):
                    at = 32 * r + NODES * copy
                    load(noderaw[at:at + NODES, :], node_w, raw_loaded)
                    load(nb[at:at + NODES, :], node_b.rearrange("(n o) -> n o", o=1), raw_loaded)
                load(b1raw[HT * r:HT * (r + 1), :], b1_d.rearrange("(t a) h -> t (a h)", a=2), raw_loaded)
                for k in range(PARTS):
                    load(b2raw[LEAVES * k:LEAVES * (k + 1), r, :], b2_d, raw_loaded)
            for r in range(BR):
                node_w, node_b, w1_d, b1_d, w2_d, b2_d = ffn[r]
                for k in range(KC):
                    load(w1[:, r, k, :].rearrange("p (l h) -> p l h", l=LEAVES),
                         w1_d[:, P * k:P * (k + 1), :].rearrange("l p h -> p l h"), ffn_loaded)
                load(w2[:, r, :, :], w2_d.rearrange("(t a) h d -> (a h) t d", a=2), ffn_loaded)
            sp.wait_ge(bias_split, 1)
            sp.wait_ge(pool_setup, 2)
            for k in range(PARTS):
                load(mk[SK + k:SK + k + 1, :, :], b1p[k], bias_rows)
                load(b2s[LEAVES * k:LEAVES * (k + 1), :, :], b2p[k][LEAVES * k:LEAVES * (k + 1)], bias_rows)

            def stack(b, after=None):
                if after is not None:
                    sp.wait_ge(pv_done, after)
                for s in range(3):
                    sp.wait_ge(parts_done, 3 * b + s + 1)
                    for n, (qp, kp) in enumerate(PAIRS):
                        rows = slice(DH * n, DH * (n + 1))
                        if s == 0:
                            for f in range(2):
                                load(qs[rows, 8 * f:8 * (f + 1), :],
                                     parts[:, qp, 0, N * f:N * (f + 1)], stacked)
                        else:
                            load(ks[rows, 8 * (s - 1):8 * s, :],
                                 parts[:, kp, s, :], stacked)

            def max_rows(at, g):
                sp.wait_ge(a_done, RING_A.count(at, ("m", g)))
                for k in range(2):
                    load(qs[SK + k:SK + k + 1, HG * g:HG * (g + 1), :],
                         mrow[HG * k:HG * (k + 1), :], mrow_stacked)

            def store(at):
                sp.wait_ge(d_done, RING_D.count(at, ("y", 1)))
                load(rows_of(out, at[1]), res[:, :, :], stored)

            stack(0)
            max_rows(("before", 0), 0)
            with sp.Fori(0, B - 1) as b:
                at = ("batch", b)
                sp.wait_ge(res_done, b + 1)
                sp.wait_ge(xn_done, b + 1)
                load(x_in[:, :, :], rows_of(x, b + 1), x_loaded)
                sp.wait_ge(pv_done, UNITS * b + 1)
                load(ctx_in[:, :, :], rows_of(ctx, b + 1), ctx_loaded)
                for g in range(1, G):
                    max_rows(at, g)
                stack(b + 1, after=UNITS * (b + 1))
                max_rows(at, 0)
                store(at)
            for g in range(1, G):
                max_rows(("last", B - 1), g)
            store(("last", B - 1))
            sp.wait_ge(stored, 16 * B)

        @block.gpsimd
        def _(pool):
            for n, (dst, value) in enumerate(((noderaw, 0.0), (nb[:, :], 0.0))):
                pool.memset(dst, value).then_inc(raw_zeroed, 1)
                pool.wait_ge(raw_zeroed, n + 1)
            for n, (dst, value) in enumerate((
                    (mk[SK:P, :, :], 0.0), (ohm[SK:P, :, :], 0.0), (ohm[SK:SK + 1, :, :], 1.0),
                    (gates[SK:P, :], 1.0), (ks[SK:SK + 2, :, :], 1.0), (v_sb[:, :, :, DH:VW], 1.0),
                    (half[:, :], -0.5))):
                pool.memset(dst, value).then_inc(pool_setup, 1)
                pool.wait_ge(pool_setup, n + 1)

            def rstd_1(b):
                pool.wait_ge(var1, b + 1)
                pool.tensor_tensor(rstd[:, :], ve[:, :], half[:, :], ALU.pow).then_inc(rstd1_done, 1)

            def rstd_2(b):
                pool.wait_ge(var2, b + 1)
                pool.tensor_tensor(rstd2[:, :], ve2[:, :], half[:, :], ALU.pow).then_inc(rstd2_done, 1)

            def residual(b, stores=None):
                if stores is not None:
                    pool.wait_ge(stored, stores)
                pool.wait_ge(x_loaded, 16 * (b + 1))
                for t in range(T):
                    last = pool.tensor_tensor(res[:, t, :], x_in[:, t, :], bias[:, :], ALU.add)
                last.then_inc(res_done, 1)

            def causal(at, u):
                if u % JT >= T:
                    pool.wait_ge(a_done, RING_A.count(at, ("e", u, HG - 1)))
                    pool.tensor_tensor(carrier_p[:, u:u + 1], half[:, 0:1], half[:, 0:1], ALU.add)
                    c = first_column(u % JT)
                    tile = probs[:, u % 3, :, c:c + P]
                    pool.affine_select(tile, tile, [[0, HG], [1, P]], ALU.is_ge, 0.0, base=0,
                                       channel_multiplier=-1).then_inc(masked, 1)

            rstd_1(0)
            pool.wait_ge(const_loaded, 16 * 6)
            residual(0)
            with pool.Fori(0, B - 1) as b:
                for u in range(UNITS):
                    causal(("batch", b), u)
                    if u == 14:
                        rstd_1(b + 1)
                rstd_2(b)
                residual(b + 1, stores=16 * (b + 1))
            for u in range(UNITS):
                causal(("last", B - 1), u)
            rstd_2(B - 1)

        @block.scalar
        def _(act):
            def take(at, key):
                act.wait_ge(a_full, RING_A.count(at, key))
                return a_slot(at, key)

            def copy_out(at, key, dst, func=ACT.Copy, rows=P):
                act.activation(dst, take(at, key)[0:rows], func).then_inc(a_done, 1)

            def exps(at, u):
                c = first_column(u % JT)
                for h in range(HG):
                    s = take(at, ("e", u, h))
                    if h == 0 and u >= 3:
                        act.wait_ge(pv_done, UNITS * at[1] + u - 2)
                    act.activation(probs[:, u % 3, h, c:N], s[:, c:N], ACT.Exp,
                                   scale=SCALE1).then_inc(a_done, 1)

            def max_row(at, g, sent):
                s = take(at, ("m", g))
                if sent is not None:
                    act.wait_ge(mrow_stacked, 32 * sent)
                act.activation(mrow[:, :], s[0:2 * HG, 0:N // 2].bitcast(BF16), ACT.Copy).then_inc(a_done, 1)

            def attention(at):
                b = at[1]
                exps(at, 0)
                for u in range(UNITS):
                    if u < UNITS - 1:
                        exps(at, u + 1)
                    if u % JT == M_AT and u // JT < G - 1:
                        g = u // JT + 1
                        max_row(at, g, G * b + g)
                    if u % JT == JT - 1:
                        g = u // JT
                        act.wait_ge(pv_done, UNITS * b + u + 1)
                        if g > 0:
                            act.wait_ge(d_full, RING_D.count(at, ("oT", g - 1)))
                        act.activation(pv_sb[:, :], ps_o[:, :], ACT.Copy).then_inc(pv_copied, 1)

            def heads_out(at):
                for k in range(KC):
                    copy_out(at, ("dT", k), oT[:, k, :])

            def front_turned(at):
                for k in range(KC):
                    copy_out(at, ("xT", k), xnT[:, k, :])
                for k in range(KC):
                    copy_out(at, ("cT", k), cT[:, k, :])

            def front(at, b):
                for s in range(3):
                    key = FRONT_D[s]
                    act.wait_ge(d_full, RING_D.count(at, key))
                    act.activation(parts[:, 0, s, :], d_slot(at, key), ACT.Copy).then_inc(part1_done, 1)

            def feedforward(at, b):
                for k in range(KC):
                    copy_out(at, ("yT", k), yT[:, k, :])
                for r in range(BR):
                    copy_out(at, ("one", r), onehot[:, r, :], ACT.Relu, rows=48)
                for r in range(BR):
                    for t in range(HT):
                        copy_out(at, ("h", r, t), hidden[:, t, :], ACT.Relu)

            def probabilities(at, b, stacks):
                if stacks is not None:
                    act.wait_ge(stacked, stacks)
                for t in range(T):
                    s = take(at, ("x", t))
                    act.wait_ge(max2_done, T * b + t + 1)
                    act.activation(p2[:, t, :], s, ACT.Exp, bias=nmaxs[:, t:t + 1], scale=SCALE2,
                                   accum_out=sums[:, t:t + 1]).then_inc(a_done, 1)

            act.wait_ge(node_turned, 1)
            act.activation(node[:, :, :].rearrange("p k n -> p (k n)"), ps_o[:, 0:KC * 96],
                           ACT.Copy).then_inc(node_done, 1)
            front_turned(("before", 0))
            front(("before", 0), 0)
            max_row(("before", 0), 0, None)
            with act.Fori(0, B - 1) as b:
                at = ("batch", b)
                attention(at)
                front_turned(at)
                heads_out(at)
                front(at, b + 1)
                feedforward(at, b)
                probabilities(at, b, 16 * STACK_DMAS * (b + 2))
                max_row(at, 0, G * b + G)
            at = ("last", B - 1)
            attention(at)
            heads_out(at)
            feedforward(at, B - 1)
            probabilities(at, B - 1, None)

        @block.vector
        def _(dve):
            def link(at, key, ins):
                ins.then_inc(chain, 1)
                await_link(at, key)

            def await_link(at, key):
                dve.wait_ge(chain, at[1] * len(CHAIN_BATCH) + CHAIN[at[0]][key] + 1)

            def take(at, key):
                dve.wait_ge(d_full, RING_D.count(at, key))
                return d_slot(at, key)

            def done(at, key):
                dve.wait_ge(d_done, RING_D.count(at, key))

            def statistics(at, name, src, stats, both, var, signal):
                for t in range(T):
                    last = dve.bn_stats(stats[:, t, :], src[:, t, :])
                link(at, (name, 0), last)
                dve.memset(carrier_v[:, 0:1], 0.0)
                for t in range(T):
                    last = dve.bn_aggr(both[:, t, :], stats[:, t, :])
                link(at, (name, 1), last)
                dve.tensor_scalar(var[:, :], both[:, :, 1], EPS, None, ALU.add).then_inc(signal, 1)

            def normalise(src, dst, both, r, signal):
                for t in range(T):
                    last = dve.tensor_scalar(dst[:, t, :], src[:, t, :], both[:, t, 0:1], r[:, t:t + 1],
                                             ALU.subtract, ALU.mult)
                last.then_inc(signal, 1)

            def stats_1(at, b):
                dve.wait_ge(x_loaded, 16 * (b + 1))
                statistics(at, "ln1", x_in, st, mv, ve, var1)

            def normalise_1(b):
                dve.wait_ge(rstd1_done, b + 1)
                normalise(x_in, xn, mv, rstd, xn_done)

            def row_max(at, n):
                h, t = n // T, n % T
                s = take(at, ("s", n))
                dve.tensor_reduce(rowmax[:, h // HG, t, h % HG:h % HG + 1], s[:, 0:N + P * (t + 1)], AX.X,
                                  ALU.max, negate=True).then_inc(d_done, 1)
                if n % (HG * T) == HG * T - 1:
                    g = h // HG
                    done(at, ("s", n))
                    link(at, ("mx", g), dve.tensor_copy(mx2[:, g, :, 0, :], rowmax[:, g, :, :]))
                    dve.tensor_tensor(mx2[:, g, :, 1, :], rowmax[:, g, :, :], mx2[:, g, :, 0, :],
                                      ALU.subtract).then_inc(max_split, 1)

            def normalise_heads(at, g):
                s = take(at, ("oT", g))[:, 0:N].rearrange("p (t h c) -> p t h c", t=T, h=HG)
                link(at, ("oT", g), dve.reciprocal(rinv[:, g, :, :], s[:, :, :, DH]))
                dst = o_sb[:, :, HG * DH * g:HG * DH * (g + 1)].rearrange("p t (h c) -> p t h c", h=HG)
                dve.tensor_tensor(dst, s[:, :, :, 0:DH], rinv[:, g, :, :].unsqueeze(3).broadcast_to([P, T, HG, DH]),
                                  ALU.mult).then_inc(d_done, 1)

            def attention(at, more):
                b = at[1]
                for u in range(UNITS):
                    for n in (LEAD + 2 * u, LEAD + 2 * u + 1):
                        if n < STILES:
                            row_max(at, n)
                    if u % JT == 1 and u > JT:
                        normalise_heads(at, u // JT - 1)
                    if more and u == 12:
                        stats_1(at, b + 1)
                    if more and u == 16:
                        normalise_1(b + 1)
                normalise_heads(at, G - 1)

            def out_rows(at):
                b = at[1]
                dve.wait_ge(res_done, b + 1)
                for c in range(2):
                    s = take(at, ("out", c)).rearrange("p (t d) -> p t d", d=D)[:, 0:2, :]
                    rows = res[:, 2 * c:2 * c + 2, :]
                    dve.tensor_tensor(rows, rows, s, ALU.add).then_inc(d_done, 1)
                done(at, ("out", 1))
                statistics(at, "ln2", res, st2, mv2, ve2, var2)
                dve.wait_ge(rstd2_done, b + 1)
                normalise(res, y_sb, mv2, rstd2, yn_done)

            def split(at, b, pieces):
                for s in pieces:
                    key = FRONT_D[s]
                    q = take(at, key)
                    dve.wait_ge(part1_done, 3 * b + s + 1)
                    dve.tensor_tensor(rest, q, parts[:, 0, s, :], ALU.subtract).then_inc(d_done, 1)
                    done(at, key)
                    link(at, ("part", s), dve.tensor_copy(parts[:, 1, s, :], rest))
                    dve.tensor_tensor(parts[:, 2, s, :], rest, parts[:, 1, s, :], ALU.subtract).then_inc(parts_done, 1)
                    dve.wait_ge(parts_done, 3 * b + s + 1)

            def values(at):
                for c in range(2):
                    s = take(at, ("v", c)).rearrange("p (t h c) -> p t h c", t=T, h=H)
                    dve.tensor_copy(v_sb[:, T * c:T * (c + 1), :, 0:DH], s).then_inc(d_done, 1)

            def feedforward(at, more):
                b = at[1]
                s = take(at, ("node",))
                dve.tensor_scalar(g0[:, :], s[0:96, 0:N], nb[:, 0:1], 0.0, ALU.add, ALU.is_ge).then_inc(d_done, 1)
                done(at, ("node",))
                dve.tensor_scalar(gates[0:96, :], g0[:, :], flip[:, 0:1], None, ALU.not_equal).then_inc(gates_done, 1)
                for r in range(2):
                    if more and r > 0:
                        for n in lead_tiles(r):
                            row_max(at, n)
                    s = take(at, ("f", r)).rearrange("p (k n) -> p k n", k=KC)
                    dve.tensor_copy(qk2T[:, r, :, :], s).then_inc(d_done, 1)
                if more:
                    for n in lead_tiles(2):
                        row_max(at, n)
                for c in range(2):
                    s = take(at, ("f", 2 + c)).rearrange("p (t d) -> p t d", d=D)[:, 0:2, :]
                    dve.tensor_copy(v2[:, 2 * c:2 * c + 2, :], s).then_inc(d_done, 1)
                for t in range(T):
                    dve.wait_ge(a_full, RING_A.count(at, ("x", t)))
                    link(at, ("x", t), dve.tensor_reduce(nmax[:, t:t + 1], a_slot(at, ("x", t)), AX.X, ALU.max,
                                                         negate=True))
                    dve.tensor_scalar(nmaxs[:, t:t + 1], nmax[:, t:t + 1], SCALE2, None, ALU.mult).then_inc(max2_done, 1)
                for t in range(T + 1):
                    if more:
                        for n in lead_tiles(("pT", t)):
                            row_max(at, n)
                    if t < T:
                        s = take(at, ("pT", t))
                        dve.tensor_copy(p2T[:, t, :], s[:, 0:N]).then_inc(d_done, 1)
                dve.wait_ge(a_done, RING_A.count(at, ("x", T - 1)))
                link(at, ("sum",), dve.reciprocal(rs2[:, :], sums[:, :]))
                for c in range(2):
                    s = take(at, ("y", c)).rearrange("p (t d) -> p t d", d=D)
                    for k in range(2):
                        t = 2 * c + k
                        last = dve.scalar_tensor_tensor(out=res[:, t, :], in0=s[:, k, :], scalar=rs2[:, t:t + 1],
                                                        in1=res[:, t, :], op0=ALU.mult, op1=ALU.add)
                    last.then_inc(d_done, 1)

            dve.memset(ps_o[:, :], 0.0).then_inc(dve_setup, 1)
            dve.wait_ge(const_loaded, 16 * 6)
            dve.tensor_copy(identb[:, :], identf[:, :]).then_inc(dve_setup, 1)
            dve.tensor_copy(maskb[:, :], maskf).then_inc(dve_setup, 1)
            stats_1(("before", 0), 0)
            normalise_1(0)
            dve.tensor_scalar(mk[0:SK, :, :].rearrange("p t (a c) -> p (t a) c", a=2),
                              path[:, :].unsqueeze(2).broadcast_to([SK, BR * LEAVES, LEAF_W]), BIG, None,
                              ALU.mult).then_inc(dve_setup, 1)
            for k in range(PARTS):
                last = dve.tensor_copy(ohm[0:SK, :, LEAVES * k:LEAVES * (k + 1)],
                                       path[:, :].rearrange("p (r l) -> p r l", r=BR))
            last.then_inc(dve_setup, 1)
            dve.wait_ge(raw_loaded, 16 * BR * 8)
            at0 = ("before", 0)
            for name, raw, rem, p3 in (("b2", b2raw, b2rem, b2p), ("b1", b1raw, b1rem, b1p)):
                link(at0, (name, 0), dve.tensor_copy(p3[0], raw))
                link(at0, (name, 1), dve.tensor_tensor(rem, raw, p3[0], ALU.subtract))
                link(at0, (name, 2), dve.tensor_copy(p3[1], rem))
                last = dve.tensor_tensor(p3[2], rem, p3[1], ALU.subtract)
                if name == "b2":
                    link(at0, (name, 3), last)
            last.then_inc(bias_split, 1)
            split(at0, 0, range(3))
            values(at0)
            for n in range(LEAD):
                row_max(at0, n)
            with dve.Fori(0, B - 1) as b:
                at = ("batch", b)
                attention(at, True)
                split(at, b + 1, (0,))
                out_rows(at)
                split(at, b + 1, (1, 2))
                values(at)
                feedforward(at, True)
            at = ("last", B - 1)
            attention(at, False)
            out_rows(at)
            feedforward(at, False)

        @block.tensor
        def _(pe):
            def open_d(at, key):
                RING_D.wait_free(pe, at, key, d_done)
                return d_slot(at, key)

            def open_a(at, key):
                RING_A.wait_free(pe, at, key, a_done)
                return a_slot(at, key)

            def turn(dst, src, ident):
                return pe.transpose(dst, src, ident)

            def product(dst, pairs, first=True, last=True):
                for n, (w, m) in enumerate(pairs):
                    mm = pe.matmul(dst, w, m, start=first and n == 0, stop=last and n == len(pairs) - 1)
                return mm

            def tiles(t):
                return slice(P * t, P * (t + 1))

            def row_scores(at, n):
                h, t = n // T, n % T
                s = open_d(at, ("s", n))
                q = qs[0:SK, h, tiles(t)]
                pe.matmul(s[:, 0:N], q, ks[0:SK, h, 0:N], start=True, stop=True)
                c = N + P * t
                pe.matmul(s[:, N:c + P], q, ks[0:SK, h, N:c + P], start=True, stop=False)
                pe.matmul(s[:, c:c + P], identb[:, :], maskb[:, :], start=False, stop=True).then_inc(d_full, 1)

            def turn_max(at, g, b):
                pe.wait_ge(max_split, G * b + g + 1)
                s = open_a(at, ("m", g))[:, 0:N // 2].bitcast(BF16)
                for t in range(T):
                    mm = turn(s[0:2 * HG, tiles(t)], mx2[:, g, t, :, :].rearrange("p k h -> p (k h)"), identb[:, :])
                mm.then_inc(a_full, 1)

            def key_scores(at, u, heads):
                g, jt = u // JT, u % JT
                c = first_column(jt)
                if jt == 0 and heads[0] == 0:
                    pe.wait_ge(mrow_stacked, 32 * (G * at[1] + g + 1))
                for h in heads:
                    s = open_a(at, ("e", u, h))
                    pe.matmul(s[:, c:N], ks[0:SK + 2, HG * g + h, tiles(jt)], qs[0:SK + 2, HG * g + h, c:N],
                              start=True, stop=True).then_inc(a_full, 1)

            def weigh(at, u):
                g, jt = u // JT, u % JT
                c = first_column(jt)
                b = at[1]
                if jt == 0 and g > 0:
                    pe.wait_ge(pv_copied, G * b + g)
                if jt < T:
                    pe.wait_ge(a_done, RING_A.count(at, ("e", u, HG - 1)))
                else:
                    pe.wait_ge(masked, G * T * b + T * g + jt - T + 1)
                for h in range(HG):
                    mm = pe.matmul(ps_o[32 * h:32 * h + VW, c:N], v_sb[:, jt, HG * g + h, :],
                                   probs[:, u % 3, h, c:N], start=(jt == 0), stop=(jt == JT - 1))
                mm.then_inc(pv_done, 1)

            def turn_heads(at, g):
                pe.wait_ge(pv_copied, G * at[1] + g + 1)
                s = open_d(at, ("oT", g))
                for t in range(T):
                    mm = turn(s[:, tiles(t)], pv_sb[:, tiles(t)], identf[:, :])
                mm.then_inc(d_full, 1)

            def turn_rows(at, name, src):
                for k in range(KC):
                    s = open_a(at, (name, k))
                    for t in range(T):
                        mm = turn(s[:, tiles(t)], src[:, t, tiles(k)], identf[:, :])
                    mm.then_inc(a_full, 1)

            def attention(at):
                key_scores(at, 0, range(HG))
                for u in range(UNITS):
                    for k in range(2):
                        if u < UNITS - 1:
                            key_scores(at, u + 1, (2 * k, 2 * k + 1))
                        if LEAD + 2 * u + k < STILES:
                            row_scores(at, LEAD + 2 * u + k)
                    if u % JT == M_AT and u // JT < G - 1:
                        turn_max(at, u // JT + 1, at[1])
                    if u % JT == 1 and u > JT:
                        turn_heads(at, u // JT - 1)
                    weigh(at, u)
                turn_heads(at, G - 1)

            def heads_turned(at):
                pe.wait_ge(d_done, RING_D.count(at, ("oT", G - 1)))
                turn_rows(at, "dT", o_sb)

            def project_out(at):
                pe.wait_ge(a_done, RING_A.count(at, ("dT", KC - 1)))
                for c in range(2):
                    s = open_d(at, ("out", c))
                    for k2 in range(2):
                        t = 2 * c + k2
                        mm = product(s[:, D * k2:D * (k2 + 1)],
                                     [(oT[:, k, tiles(t)], wout_sb[:, k, :]) for k in range(KC)])
                    mm.then_inc(d_full, 1)

            def front_turned(at, b):
                pe.wait_ge(xn_done, b + 1)
                turn_rows(at, "xT", xn)
                pe.wait_ge(ctx_loaded, 16 * (b + 1))
                turn_rows(at, "cT", ctx_in)

            def project_q(at):
                pe.wait_ge(a_done, RING_A.count(at, ("xT", KC - 1)))
                s = open_d(at, ("q",))
                for f in range(2):
                    mm = product(s[:, N * f:N * (f + 1)],
                                 [(wq_sb[:, k, tiles(f)], xnT[:, k, :]) for k in range(KC)])
                mm.then_inc(d_full, 1)

            def project_kv(at):
                pe.wait_ge(a_done, RING_A.count(at, ("cT", KC - 1)))
                for f in range(2):
                    s = open_d(at, ("k", f))
                    for c, src in enumerate((cT, xnT)):
                        mm = product(s[:, N * c:N * (c + 1)],
                                     [(wkv_sb[:, k, tiles(f)], src[:, k, :]) for k in range(KC)])
                    mm.then_inc(d_full, 1)
                for c, src in enumerate((cT, xnT)):
                    s = open_d(at, ("v", c))
                    for t in range(T):
                        mm = product(s[:, D * t:D * (t + 1)],
                                     [(src[:, k, tiles(t)], wkv_sb[:, k, D:2 * D]) for k in range(KC)])
                    mm.then_inc(d_full, 1)

            def hidden_layer(at, r, scores=()):
                for t in range(HT):
                    s = open_a(at, ("h", r, t))
                    product(s, [(w1[:, r, k, tiles(t)], yT[:, k, :]) for k in range(KC)], last=False)
                    pe.matmul(s, mk[:, HT * r + t, :], gates[:, :], start=False, stop=True).then_inc(a_full, 1)
                    for n in scores[t:t + 1]:
                        row_scores(at, n)

            def feedforward(at, more):
                b = at[1]
                pe.wait_ge(yn_done, b + 1)
                turn_rows(at, "yT", y_sb)
                pe.wait_ge(a_done, RING_A.count(at, ("yT", KC - 1)))
                s = open_d(at, ("node",))
                product(s[0:96, 0:N], [(node[:, k, :], yT[:, k, :]) for k in range(KC)]).then_inc(d_full, 1)
                pe.wait_ge(gates_done, b + 1)
                for r in range(BR):
                    s = open_a(at, ("one", r))
                    pe.matmul(s[0:48, :], ohm[:, r, :], gates[:, :], start=True, stop=True).then_inc(a_full, 1)
                for r in range(2):
                    if more and r > 0:
                        pe.wait_ge(stacked, 16 * STACK_DMAS * (b + 2))
                    hidden_layer(at, r, lead_tiles(r) if more and r > 0 else ())
                    s = open_d(at, ("f", r))
                    for t in range(HT):
                        pe.wait_ge(a_done, RING_A.count(at, ("h", r, t)))
                        for k in range(KC):
                            pe.matmul(s[:, N * k:N * (k + 1)], w2[:, r, t, tiles(k)], hidden[:, t, :],
                                      start=(t == 0), stop=False)
                    for k in range(KC):
                        mm = pe.matmul(s[:, N * k:N * (k + 1)], b2s[:, r, tiles(k)], onehot[:, r, :],
                                       start=False, stop=True)
                    mm.then_inc(d_full, 1)
                hidden_layer(at, 2, lead_tiles(2) if more else ())
                pe.wait_ge(a_done, RING_A.count(at, ("h", 2, HT - 1)))
                for c in range(2):
                    s = open_d(at, ("f", 2 + c))
                    for k2 in range(2):
                        t = 2 * c + k2
                        mm = product(s[:, D * k2:D * (k2 + 1)],
                                     [(hidden[:, j, tiles(t)], w2[:, 2, j, :]) for j in range(HT)]
                                     + [(onehot[:, 2, tiles(t)], b2s[:, 2, :])])
                    mm.then_inc(d_full, 1)
                pe.wait_ge(d_done, RING_D.count(at, ("f", 1)))
                for t in range(T):
                    s = open_a(at, ("x", t))
                    product(s, [(qk2T[:, 0, k, tiles(t)], qk2T[:, 1, k, :]) for k in range(KC)]).then_inc(a_full, 1)
                for t in range(T + 1):
                    if more:
                        for n in lead_tiles(("pT", t)):
                            row_scores(at, n)
                    if t == 1 and more:
                        turn_max(at, 0, b + 1)
                    if t == T:
                        break
                    pe.wait_ge(a_done, RING_A.count(at, ("x", t)))
                    s = open_d(at, ("pT", t))
                    for j in range(T):
                        mm = turn(s[:, tiles(j)], p2[:, t, tiles(j)], identf[:, :])
                    mm.then_inc(d_full, 1)
                pe.wait_ge(d_done, RING_D.count(at, ("pT", T - 1)))
                for c in range(2):
                    s = open_d(at, ("y", c))
                    for k2 in range(2):
                        t = 2 * c + k2
                        mm = product(s[:, D * k2:D * (k2 + 1)],
                                     [(p2T[:, t, tiles(j)], v2[:, j, :]) for j in range(T)])
                    mm.then_inc(d_full, 1)

            pe.wait_ge(raw_loaded, 16 * BR * 8)
            pe.wait_ge(const_loaded, 16 * 6)
            pe.wait_ge(dve_setup, 3)
            for k in range(KC):
                mm = turn(ps_o[:, 96 * k:96 * (k + 1)], noderaw[:, tiles(k)], identf[0:96, 0:96])
            mm.then_inc(node_turned, 1)
            pe.wait_ge(wqkv_loaded, 32)
            front_turned(("before", 0), 0)
            project_q(("before", 0))
            project_kv(("before", 0))
            pe.wait_ge(stacked, 16 * STACK_DMAS)
            pe.wait_ge(pool_setup, 7)
            for n in range(LEAD):
                row_scores(("before", 0), n)
            turn_max(("before", 0), 0, 0)
            pe.wait_ge(node_done, 1)
            pe.wait_ge(dve_setup, 5)
            pe.wait_ge(bias_rows, 16 * 2 * PARTS)
            pe.wait_ge(ffn_loaded, 16 * BR * (KC + 1))
            with pe.Fori(0, B - 1) as b:
                at = ("batch", b)
                attention(at)
                front_turned(at, b + 1)
                heads_turned(at)
                project_q(at)
                project_out(at)
                project_kv(at)
                feedforward(at, True)
            attention(("last", B - 1))
            heads_turned(("last", B - 1))
            project_out(("last", B - 1))
            feedforward(("last", B - 1), False)


def constants():
    import numpy as np

    ident = np.eye(P, dtype=np.float32)
    mask = np.where(np.arange(P)[None, :] > np.arange(P)[:, None], np.float32(-BIG), np.float32(0))
    path = np.zeros((96, BR * LEAVES), np.float32)
    flip = np.zeros((96, 1), np.float32)
    for r in range(BR):
        flip[32 * r + NODES:32 * r + 2 * NODES] = 1
        for leaf in range(LEAVES):
            node = leaf + NODES
            while node:
                right, node = (node - 1) % 2, (node - 1) // 2
                path[32 * r + node + (NODES if right else 0), r * LEAVES + leaf] = -1
    return {"c_ident": ident, "c_mask": mask.astype(np.float32), "c_path": path, "c_flip": flip}


_FFN = ["node_w", "node_b", "w1", "b1", "w2", "b2"]
_INS = (["x", "ctx_1024", "L0_xattn_Wq", "L0_xattn_Wkv", "L0_xattn_Wout", "L0_xattn_bout"]
        + [f"L0_ffn_{r}_{n}" for r in "qkv" for n in _FFN])


def by_column(w):
    return w.reshape(D, 2, H // 2, DH).transpose(0, 1, 3, 2).reshape(D, D)


def kernel(**inputs):
    import numpy as _np
    import concourse.bacc as _bacc
    from concourse import mybir as _mybir
    from concourse.bass_utils import run_bass_kernel_spmd as _run

    nc = _bacc.Bacc("TRN2", target_bir_lowering=False, num_devices=1)
    arrays, args = {}, []
    consts = constants()
    for name in _INS + list(consts):
        a = _np.asarray(inputs[name] if name in inputs else consts[name])
        if name == "L0_xattn_Wq":
            a = by_column(a)
        if name == "L0_xattn_Wkv":
            a = _np.concatenate([by_column(a[:, :D]), a[:, D:]], axis=1)
        a = _np.ascontiguousarray(a)
        arrays[f"in_{name}_dram"] = a
        args.append(nc.dram_tensor(f"in_{name}_dram", a.shape, _mybir.dt.from_np(a.dtype), kind="ExternalInput").ap())
    out = nc.dram_tensor("out_0_dram", (B, N, D), _mybir.dt.float32, kind="ExternalOutput").ap()
    ffn = [args[6 + 6 * r:12 + 6 * r] for r in range(BR)]
    program(nc, *args[:6], ffn, *args[24:28], out)
    r = _run(nc, [arrays], core_ids=[0])
    return r.results[0]["out_0_dram"]
```

```python
from contextlib import ExitStack

import concourse.bass as bass
from concourse import mybir

F32 = mybir.dt.float32
F32R = mybir.dt.float32r
BF16 = mybir.dt.bfloat16
ALU = mybir.AluOpType
ACT = mybir.ActivationFunctionType
AX = mybir.AxisListType

P = 128
B, N, D = 8, 512, 256
H = 16
DH = D // H
HG = 4
G = H // HG
T = N // P
KC = D // P
J = 2 * N
JT = J // P
LEAVES, LEAF_W, NODES = 16, 64, 15
BR = 3
HID = LEAVES * LEAF_W
HT = HID // P
PARTS = 3
PAIRS = ((0, 0), (0, 1), (1, 0), (1, 1), (0, 2), (2, 0))
SK = len(PAIRS) * DH
VW = DH + 1
BIG = 1e30
EPS = 1e-5
SCALE1 = float(DH) ** -0.5
SCALE2 = float(D) ** -0.5

UNITS = G * JT
STILES = H * T
LEAD = 28
S_PER_UNIT = (3, 2, 2, 2, 2, 2, 1, 1)
TAIL = STILES - G * sum(S_PER_UNIT)
STACK = 2 * len(PAIRS)
M_AT = 4

FRONT = [("xT",), ("cT",), ("q",), ("k", 0), ("k", 1), ("v", 0), ("v", 1)]
FRONT_AT = {8: ("xT",), 9: ("cT",), 10: ("q",), 11: ("k", 0), 12: ("k", 1)}
STATS_AT, NORM_AT = 5, 7


def row_tiles(n, count, more):
    tiles = [divmod(m, STILES) for m in range(n, n + count)]
    return [(k, m) for k, m in tiles if k == 0 or more]


def unit_tiles(u, more):
    return row_tiles(LEAD + sum(S_PER_UNIT) * (u // JT) + sum(S_PER_UNIT[:u % JT]), S_PER_UNIT[u % JT], more)


def tail_tiles(part):
    return row_tiles(STILES + LEAD - TAIL + TAIL // 2 * part, TAIL // 2, True)


def uses_d(more):
    keys = []
    for u in range(UNITS):
        keys += [("s",) + n for n in unit_tiles(u, more)]
        if u % JT == 1 and u > JT:
            keys += [("oT", u // JT - 1)]
        if more and u in FRONT_AT:
            keys += [FRONT_AT[u]]
    if not more:
        return keys + [("oT", G - 1), ("dT",), ("out", 0), ("out", 1)]
    return (keys + [("v", 0), ("oT", G - 1), ("v", 1)] + [("s",) + n for n in tail_tiles(0)] + [("dT",)]
            + [("s",) + n for n in tail_tiles(1)] + [("out", 0), ("out", 1)])


def uses_a(more):
    keys = []
    for u in range(UNITS):
        if u + 1 < UNITS or more:
            keys += [("e", (u + 1) % UNITS, h) for h in range(HG)]
        if u % JT == M_AT and (u // JT + 1 < G or more):
            keys += [("m", (u // JT + 1) % G)]
    return keys


def chain_steps(where):
    def mx(n):
        return [("mx", n[0], n[1] // (HG * T))] if n[1] % (HG * T) == HG * T - 1 else []

    if where == "before":
        steps = [("ln", 0), ("ln", 1)]
        steps += [("b2", 0), ("b2", 1), ("b2", 2), ("b2", 3), ("b1", 0), ("b1", 1), ("b1", 2)]
        for n in range(LEAD):
            steps += mx((0, n))
        return steps
    more, steps = where == "batch", []
    for u in range(UNITS):
        for n in unit_tiles(u, more):
            steps += mx(n)
        if u % JT == 1 and u > JT:
            steps += [("oT", u // JT - 1)]
        if more and u == STATS_AT:
            steps += [("ln", 0), ("ln", 1)]
    steps += [("oT", G - 1)]
    if more:
        for n in tail_tiles(0) + tail_tiles(1):
            steps += mx(n)
    return steps


class Order:

    def __init__(self, before, batch, last):
        self.per, first = len(batch), len(before)
        self.number = {"before": {key: n for n, key in enumerate(before)},
                       "batch": {key: first + n for n, key in enumerate(batch)},
                       "last": {key: first + n for n, key in enumerate(last)}}
        for where, keys in (("before", before), ("batch", batch), ("last", last)):
            assert len(self.number[where]) == len(keys), where

    def count(self, at, key):
        return at[1] * self.per + self.number[at[0]][key] + 1


class Ring(Order):

    def __init__(self, slots, *uses):
        super().__init__(*uses)
        self.slots = slots
        assert self.per % slots == 0, self.per

    def slot(self, at, key):
        return self.number[at[0]][key] % self.slots

    def wait_free(self, engine, at, key, emptied, source=None):
        number = self.number[at[0]]
        if source is not None and number[source] > number[key] - self.slots:
            engine.wait_ge(emptied, self.count(at, source))
        elif number[key] >= self.slots:
            engine.wait_ge(emptied, self.count(at, key) - self.slots)


RING_D = Ring(2, FRONT + [("s", 0, n) for n in range(LEAD)], uses_d(True), uses_d(False))
RING_A = Ring(3, [("m", 0)] + [("e", 0, h) for h in range(HG)], uses_a(True), uses_a(False))
CHAIN = Order(*(chain_steps(where) for where in ("before", "batch", "last")))

TURN_Y = [("yT", k) for k in range(KC)]
ONES = [("one", r) for r in range(BR)]


def uses_h(more):
    return ([("h", r, t) for r in range(BR) for t in range(HT)] + (TURN_Y if more else [])
            + [("pT", t) for t in range(T)] + (ONES if more else []))


def uses_f(more):
    return [("f", r) for r in range(BR)] + ([("node",)] if more else []) + [("y", 0), ("y", 1)]


def highs(uses):
    return [key for key in uses if key[0] in ("h", "yT", "pT")]


RING_H = Ring(3, TURN_Y + ONES, uses_h(True), uses_h(False))
HIGH_H = Order(*(highs(uses) for uses in (TURN_Y, uses_h(True), uses_h(False))))
RING_F = Ring(2, [("node",)], uses_f(True), uses_f(False))


def links_2(more):
    ln = [("ln", 0), ("ln", 1)]
    return (ln if more else []) + [("x", t) for t in range(T)] + [("sum",)]


CHAIN2 = Order([("ln", 0), ("ln", 1)], links_2(True), links_2(False))


def program(nc, x, ctx, wq, wkv, wout, bout, ffn, c_ident, c_mask, c_path, c_flip, out):
    keep = ExitStack()
    with keep:
        def sem(name):
            return keep.enter_context(nc.semaphore(name))

        def sb(name, shape, dt=F32):
            return keep.enter_context(nc.sbuf_tensor(name, shape, dt))

        x1_dram = nc.dram_tensor("x1_dram", (B, N, D), F32, kind="Internal").ap()

        w1q = sb("w1q", [P, 2, KC, HID], F32R)
        w2q = sb("w2q", [P, 2, HT, D], F32R)
        mk = sb("mk", [P, BR * HT, P], BF16)
        ohm = sb("ohm", [P, BR, 48], BF16)
        b2s = sb("b2s", [48, BR, D], BF16)
        node = sb("node", [P, 2, KC, 96], F32R)
        identf = sb("identf", [P, P])
        flip = sb("flip", [96, 1])
        nb = sb("nb", [96, 1])
        gates = sb("gates", [P, N], BF16)
        half = sb("half", [P, T])
        carrier_v = sb("carrier_v", [P, 1])
        st, mv = sb("st", [P, T, 6]), sb("mv", [P, T, 2])
        ve, rstd = sb("ve", [P, T]), sb("rstd", [P, T])
        work = sb("work", [P, 7 * T * D])
        raw2 = [work[:, 2048 * n:2048 * (n + 1)] for n in (0, 1, 2, 0)]

        ps_d = keep.enter_context(nc.psum_tensor("ps_d", [P, 2, 1024], F32))
        ps_a = keep.enter_context(nc.psum_tensor("ps_a", [P, 3, 512], F32))
        ps_o = keep.enter_context(nc.psum_tensor("ps_o", [P, 512], F32))

        d_full, d_done = sem("d_full"), sem("d_done")
        a_full, a_done = sem("a_full"), sem("a_done")
        h_full, h_done = sem("h_full"), sem("h_done")
        f_full, f_done = sem("f_full"), sem("f_done")
        h_high, f_high = sem("h_high"), sem("f_high")
        x_loaded, ctx_loaded = sem("x_loaded"), sem("ctx_loaded")
        wq_loaded, wkv_loaded, wout_loaded = sem("wq_loaded"), sem("wkv_loaded"), sem("wout_loaded")
        w1q_loaded, w2q_loaded = sem("w1q_loaded"), sem("w2q_loaded")
        ident_loaded, const_loaded, raw_loaded = sem("ident_loaded"), sem("const_loaded"), sem("raw_loaded")
        raw_zeroed, pool_setup, dve_setup = sem("raw_zeroed"), sem("pool_setup"), sem("dve_setup")
        w_high, w_split = sem("w_high"), sem("w_split")
        bias_split, bias_rows = sem("bias_split"), sem("bias_rows")
        node_turned, node_high, node_done = sem("node_turned"), sem("node_high"), sem("node_done")
        var1, rstd1_done, xn_done, res_done = sem("var1"), sem("rstd1_done"), sem("xn_done"), sem("res_done")
        front_high, heads_high = sem("front_high"), sem("heads_high")
        part1_done, part2_done, parts_done = sem("part1_done"), sem("part2_done"), sem("parts_done")
        stacked = [sem(f"stacked{g}") for g in range(G)]
        max_split, mrow_stacked = sem("max_split"), sem("mrow_stacked")
        masked, pv_done, pv_copied = sem("masked"), sem("pv_done"), sem("pv_copied")
        x1_stored = sem("x1_stored")
        chain, chain2 = sem("chain"), sem("chain2")
        raw2_loaded, w2_high, w2_split = sem("raw2_loaded"), sem("w2_high"), sem("w2_split")
        last_loaded = sem("last_loaded")
        x_full, x_max, x_done = sem("x_full"), sem("x_max"), sem("x_done")
        x1_loaded, x1_moved = sem("x1_loaded"), sem("x1_moved")
        var2, rstd2_done, yn_done, gates_done = sem("var2"), sem("rstd2_done"), sem("yn_done"), sem("gates_done")
        stored = sem("stored")

        def first_column(jt):
            return 0 if jt < T else P * (jt - T)

        def rows_of(array, b):
            return array[bass.ds(b, 1)].rearrange("o (t p) d -> p (o t) d", p=P)

        def tiles(t):
            return slice(P * t, P * (t + 1))

        def flat(array):
            return array.rearrange("p a b -> p (a b)")

        def both(array, *index):
            return tuple(array[(slice(None), part) + index] for part in (0, 1))

        def product(pe, dst, pairs, first=True, last=True):
            passes = [(w[i], m[j]) for w, m in pairs for i, j in ((1, 0), (0, 1), (0, 0))]
            for n, (w, m) in enumerate(passes):
                mm = pe.matmul(dst, w, m, start=first and n == 0, stop=last and n == len(passes) - 1)
            return mm

        def turn_rows(pe, dst, src):
            for k in range(KC):
                for t in range(T):
                    mm = pe.transpose(dst[:, N * k + P * t:N * k + P * (t + 1)], src[:, t, tiles(k)], identf[:, :])
            return mm

        def low_part(dve, low, src, high):
            return dve.tensor_tensor(low, src, high.bitcast(F32), ALU.subtract)

        def statistics(dve, src, var, signal, steps, at, link):
            for t in range(T):
                last = dve.bn_stats(st[:, t, :], src[:, t, :])
            link(at, ("ln", 0), last)
            dve.memset(carrier_v[:, 0:1], 0.0)
            for t in range(T):
                last = dve.bn_aggr(mv[:, t, :], st[:, t, :])
            link(at, ("ln", 1), last)
            dve.tensor_scalar(var[:, :], mv[:, :, 1], EPS, None, ALU.add).then_inc(signal, 1)

        def normalise(dve, src, dst, signal):
            for t in range(T):
                last = dve.tensor_scalar(dst[:, t, :], src[:, t, :], mv[:, t, 0:1], rstd[:, t:t + 1],
                                         ALU.subtract, ALU.mult)
            last.then_inc(signal, 1)

        with ExitStack() as es:
            def sb1(name, shape, dt=F32):
                return es.enter_context(nc.sbuf_tensor(name, shape, dt))

            parts = work[:, 0:4608].bitcast(BF16).rearrange("p (c s n) -> p c s n", c=PARTS, s=3)
            x_in = work[:, 4608:5632].rearrange("p (t d) -> p t d", t=T)
            xn = work[:, 5632:6656].rearrange("p (t d) -> p t d", t=T)
            ctx_in = sb1("ctx_in", [P, T, D])
            res = sb1("res", [P, T, D])
            xnT = sb1("xnT", [P, 2, KC, N], F32R)
            cT = sb1("cT", [P, 2, KC, N], F32R)
            oT = cT
            o_sb = sb1("o_sb", [P, T, D])
            pv_sb = sb1("pv_sb", [P, N])
            rest = sb1("rest", [P, J])
            qs = sb1("qs", [P, H, N], BF16)
            ks = sb1("ks", [P, H, J], BF16)
            v_sb = sb1("v_sb", [P, JT, H, VW])
            shared = sb1("shared", [P, 3 * HG * N])
            probs = shared[:, :].rearrange("p (s h n) -> p s h n", s=3, h=HG)
            wq_sb = sb1("wq_sb", [P, 2, KC, D], F32R)
            wkv_sb = sb1("wkv_sb", [P, 2, KC, 2 * D], F32R)
            wout_sb = sb1("wout_sb", [P, 2, KC, D], F32R)
            identb = sb1("identb", [P, P], BF16)
            maskb = sb1("maskb", [P, P], BF16)
            bias = sb1("bias", [P, D])
            path = sb1("path", [96, BR * LEAVES])
            rowmax = sb1("rowmax", [P, G, T, HG])
            mx2 = sb1("mx2", [P, G, T, 2, HG], BF16)
            mrow = sb1("mrow", [2 * HG, N], BF16)
            rinv = sb1("rinv", [P, G, T, HG])
            carrier_p = sb1("carrier_p", [P, UNITS])
            raw_q, raw_kv, raw_out, raw_ffn = (shared[:, 0:512], shared[:, 512:1536], shared[:, 1536:2048],
                                               shared[:, 2048:4096])
            b2raw = shared[0:48, 4096:4864].rearrange("p (r d) -> p r d", r=BR)
            b2rem = shared[0:48, 4864:5632].rearrange("p (r d) -> p r d", r=BR)
            o_flat = flat(o_sb[:, :, :])
            b2p = [area.bitcast(BF16).rearrange("p (r d) -> p r d", r=BR)
                   for area in (shared[0:48, 5632:6016], o_flat[0:48, 256:640], o_flat[0:48, 640:1024])]
            maskf = shared[:, 6016:6144]
            noderaw = o_flat[0:96, 0:D]
            b1raw, b1rem = pv_sb[0:BR * HT, 0:P], pv_sb[0:BR * HT, P:2 * P]
            b1p = [pv_sb[0:BR * HT, 256 + 64 * k:320 + 64 * k].bitcast(BF16) for k in range(PARTS)]
            weights = [(raw_q, wq_sb, wq_loaded), (raw_kv, wkv_sb, wkv_loaded), (raw_out, wout_sb, wout_loaded),
                       (raw_ffn, w1q, w1q_loaded), (raw_ffn, w2q, w2q_loaded)]

            def d_slot(at, key):
                return ps_d[:, RING_D.slot(at, key), :]

            def a_slot(at, key):
                return ps_a[:, RING_A.slot(at, key), :]

            block = es.enter_context(nc.Block())

            @block.sync
            def _(sp):
                def load(dst, src, signal):
                    sp.dma_start(dst, src).then_inc(signal, 16)

                load(x_in, rows_of(x, 0), x_loaded)
                load(identf[:, :], c_ident, ident_loaded)
                load(ctx_in[:, :, :], rows_of(ctx, 0), ctx_loaded)
                load(raw_q.rearrange("p (k n) -> p k n", k=KC), wq.rearrange("(k p) n -> p k n", p=P), wq_loaded)
                load(raw_kv.rearrange("p (k n) -> p k n", k=KC), wkv.rearrange("(k p) n -> p k n", p=P), wkv_loaded)
                load(maskf, c_mask, const_loaded)
                load(path[:, :], c_path, const_loaded)
                load(flip[:, :], c_flip, const_loaded)
                load(bias[:, :], bout.partition_broadcast(P), const_loaded)
                sp.wait_ge(raw_zeroed, 2)
                for r in range(BR):
                    node_w, node_b, w1_d, b1_d, w2_d, b2_d = ffn[r]
                    for copy in range(2):
                        at = 32 * r + NODES * copy
                        load(noderaw[at:at + NODES, :], node_w, raw_loaded)
                        load(nb[at:at + NODES, :], node_b.rearrange("(n o) -> n o", o=1), raw_loaded)
                    load(b1raw[HT * r:HT * (r + 1), :], b1_d.rearrange("(t a) h -> t (a h)", a=2), raw_loaded)
                    for k in range(PARTS):
                        load(b2raw[LEAVES * k:LEAVES * (k + 1), r, :], b2_d, raw_loaded)

                def load_w1(dst, r, signal):
                    for k in range(KC):
                        load(dst[:, HID * k:HID * (k + 1)].rearrange("p (l h) -> p l h", l=LEAVES),
                             ffn[r][2][:, P * k:P * (k + 1), :].rearrange("l p h -> p l h"), signal)

                def load_w2(dst, r, signal):
                    load(dst.rearrange("p (t d) -> p t d", t=HT),
                         ffn[r][4].rearrange("(t a) h d -> (a h) t d", a=2), signal)

                load(raw_out.rearrange("p (k n) -> p k n", k=KC), wout.rearrange("(k p) n -> p k n", p=P), wout_loaded)
                load_w1(raw_ffn, 0, w1q_loaded)
                sp.wait_ge(bias_split, 1)
                sp.wait_ge(pool_setup, 2)
                for k in range(PARTS):
                    load(mk[SK + k:SK + k + 1, :, :], b1p[k], bias_rows)
                    load(b2s[LEAVES * k:LEAVES * (k + 1), :, :], b2p[k][LEAVES * k:LEAVES * (k + 1)], bias_rows)

                def stack(g):
                    rows = slice(HG * DH * (g % 2), HG * DH * (g % 2 + 1))
                    heads = slice(HG * g, HG * (g + 1))
                    for n, (qp, kp) in enumerate(PAIRS):
                        terms = slice(DH * n, DH * (n + 1))
                        f = g // 2
                        load(qs[terms, heads, :], parts[rows, qp, 0, N * f:N * (f + 1)], stacked[g])
                        load(ks[terms, heads, :], parts[rows, kp, 1 + f, :], stacked[g])

                def max_rows(at, g):
                    sp.wait_ge(a_done, RING_A.count(at, ("m", g)))
                    for k in range(2):
                        load(qs[SK + k:SK + k + 1, HG * g:HG * (g + 1), :],
                             mrow[HG * k:HG * (k + 1), :], mrow_stacked)

                def store(at):
                    sp.wait_ge(d_done, RING_D.count(at, ("out", 1)))
                    load(rows_of(x1_dram, at[1]), res[:, :, :], x1_stored)

                for g in range(G):
                    sp.wait_ge(parts_done, 2 + g // 2)
                    stack(g)
                sp.wait_ge(w_split, 4)
                load_w2(raw_ffn, 0, w2q_loaded)
                max_rows(("before", 0), 0)
                with sp.Fori(0, B - 1) as b:
                    at = ("batch", b)
                    sp.wait_ge(res_done, b + 1)
                    sp.wait_ge(xn_done, b + 1)
                    load(x_in, rows_of(x, b + 1), x_loaded)
                    sp.wait_ge(pv_done, UNITS * b + 1)
                    load(ctx_in[:, :, :], rows_of(ctx, b + 1), ctx_loaded)
                    max_rows(at, 1)
                    max_rows(at, 2)
                    sp.wait_ge(parts_done, 3 * b + 5)
                    stack(0)
                    sp.wait_ge(pv_done, UNITS * b + 2 * JT)
                    stack(1)
                    max_rows(at, 3)
                    sp.wait_ge(pv_done, UNITS * b + 3 * JT)
                    stack(2)
                    max_rows(at, 0)
                    sp.wait_ge(pv_done, UNITS * b + 4 * JT)
                    stack(3)
                    store(at)
                at = ("last", B - 1)
                for g in range(G):
                    sp.wait_ge(stacked[g], 16 * STACK * B)
                sp.wait_ge(res_done, B)
                sp.wait_ge(pv_done, UNITS * (B - 1) + 1)
                load_w1(raw2[0], 1, raw2_loaded)
                load_w2(raw2[1], 1, raw2_loaded)
                load_w1(raw2[2], 2, raw2_loaded)
                for g in range(1, G):
                    max_rows(at, g)
                store(at)
                sp.wait_ge(x1_stored, 16 * B)

            @block.gpsimd
            def _(pool):
                for n, (dst, value) in enumerate(((noderaw, 0.0), (nb[:, :], 0.0))):
                    pool.memset(dst, value).then_inc(raw_zeroed, 1)
                    pool.wait_ge(raw_zeroed, n + 1)
                for n, (dst, value) in enumerate((
                        (mk[SK:P, :, :], 0.0), (ohm[SK:P, :, :], 0.0), (ohm[SK:SK + 1, :, :], 1.0),
                        (gates[SK:P, :], 1.0), (ks[SK:SK + 2, :, :], 1.0), (v_sb[:, :, :, DH:VW], 1.0),
                        (half[:, :], -0.5))):
                    pool.memset(dst, value).then_inc(pool_setup, 1)
                    pool.wait_ge(pool_setup, n + 1)

                def rstd_1(b):
                    pool.wait_ge(var1, b + 1)
                    pool.tensor_tensor(rstd[:, :], ve[:, :], half[:, :], ALU.pow).then_inc(rstd1_done, 1)

                def residual(b, stores=None):
                    if stores is not None:
                        pool.wait_ge(x1_stored, stores)
                    pool.wait_ge(x_loaded, 16 * (b + 1))
                    for t in range(T):
                        last = pool.tensor_tensor(res[:, t, :], x_in[:, t, :], bias[:, :], ALU.add)
                    last.then_inc(res_done, 1)

                def causal(at, u):
                    if u % JT >= T:
                        pool.wait_ge(a_done, RING_A.count(at, ("e", u, HG - 1)))
                        pool.tensor_tensor(carrier_p[:, u:u + 1], half[:, 0:1], half[:, 0:1], ALU.add)
                        c = first_column(u % JT)
                        tile = probs[:, u % 3, :, c:c + P]
                        pool.affine_select(tile, tile, [[0, HG], [1, P]], ALU.is_ge, 0.0, base=0,
                                           channel_multiplier=-1).then_inc(masked, 1)

                def third_part(b, n):
                    pool.wait_ge(part2_done, 3 * b + n + 1)
                    pool.tensor_tensor(parts[:, 2, n, :], rest[:, :], parts[:, 1, n, :],
                                       ALU.subtract).then_inc(parts_done, 1)

                rstd_1(0)
                for n in range(3):
                    third_part(0, n)
                pool.wait_ge(const_loaded, 16 * 4)
                residual(0)
                with pool.Fori(0, B - 1) as b:
                    for u in range(UNITS):
                        causal(("batch", b), u)
                        if FRONT_AT.get(u, ("",))[0] in ("q", "k"):
                            third_part(b + 1, FRONT.index(FRONT_AT[u]) - 2)
                        if u == STATS_AT + 1:
                            rstd_1(b + 1)
                    residual(b + 1, stores=16 * (b + 1))
                for u in range(UNITS):
                    causal(("last", B - 1), u)

            @block.scalar
            def _(act):
                def high(at, key, dst, signal):
                    act.wait_ge(d_full, RING_D.count(at, key))
                    act.activation(dst, d_slot(at, key), ACT.Copy).then_inc(signal, 1)

                def weight_high(n):
                    raw, split, loaded = weights[n]
                    act.wait_ge(loaded, 32 if loaded is w1q_loaded else 16)
                    act.activation(flat(split[:, 0, :, :]), raw, ACT.Copy).then_inc(w_high, 1)

                def exps(at, u):
                    own, u, later = at, u % UNITS, u // UNITS
                    c = first_column(u % JT)
                    for h in range(HG):
                        act.wait_ge(a_full, RING_A.count(own, ("e", u, h)))
                        if h == 0 and (u >= 3 or later):
                            act.wait_ge(pv_done, UNITS * (at[1] + later) + (u - 2 if u >= 3 else -1))
                        act.activation(probs[:, u % 3, h, c:N], a_slot(own, ("e", u, h))[:, c:N], ACT.Exp,
                                       scale=SCALE1).then_inc(a_done, 1)

                def max_row(at, g, sent):
                    act.wait_ge(a_full, RING_A.count(at, ("m", g)))
                    if sent is not None:
                        act.wait_ge(mrow_stacked, 32 * sent)
                    act.activation(mrow[:, :], a_slot(at, ("m", g))[0:2 * HG, 0:N // 2].bitcast(BF16),
                                   ACT.Copy).then_inc(a_done, 1)

                def front(at, key):
                    if key == ("xT",):
                        high(at, key, flat(xnT[:, 0, :, :]), front_high)
                    elif key == ("cT",):
                        high(at, key, flat(cT[:, 0, :, :]), front_high)
                    elif key[0] in ("q", "k"):
                        high(at, key, parts[:, 0, FRONT.index(key) - 2, :], part1_done)

                def attention(at, more):
                    b = at[1]
                    for u in range(UNITS):
                        if u + 1 < UNITS or more:
                            exps(at, u + 1)
                        if u % JT == M_AT and (u // JT + 1 < G or more):
                            g = u // JT + 1
                            max_row(at, g % G, G * b + g)
                        if more and u in FRONT_AT:
                            front(at, FRONT_AT[u])
                        if u % JT == JT - 1:
                            g = u // JT
                            act.wait_ge(pv_done, UNITS * b + u + 1)
                            if g > 0:
                                act.wait_ge(d_full, RING_D.count(at, ("oT", g - 1)))
                            act.activation(pv_sb[:, :], ps_o[:, :], ACT.Copy).then_inc(pv_copied, 1)
                    high(at, ("dT",), flat(oT[:, 0, :, :]), heads_high)

                at0 = ("before", 0)
                weight_high(0)
                weight_high(1)
                for key in FRONT:
                    front(at0, key)
                act.wait_ge(node_turned, 1)
                act.activation(node[:, 0, :, :].rearrange("p k n -> p (k n)"), ps_o[:, 0:KC * 96],
                               ACT.Copy).then_inc(node_high, 1)
                for n in range(2, 5):
                    weight_high(n)
                max_row(at0, 0, None)
                for h in range(HG):
                    act.wait_ge(a_full, RING_A.count(at0, ("e", 0, h)))
                    act.activation(probs[:, 0, h, :], a_slot(at0, ("e", 0, h)), ACT.Exp,
                                   scale=SCALE1).then_inc(a_done, 1)
                with act.Fori(0, B - 1) as b:
                    attention(("batch", b), True)
                attention(("last", B - 1), False)

            @block.vector
            def _(dve):
                def link(at, key, ins):
                    ins.then_inc(chain, 1)
                    dve.wait_ge(chain, CHAIN.count(at, key))

                def take(at, key):
                    dve.wait_ge(d_full, RING_D.count(at, key))
                    return d_slot(at, key)

                def done(at, key):
                    dve.wait_ge(d_done, RING_D.count(at, key))

                def weight_low(n):
                    raw, split, loaded = weights[n]
                    dve.wait_ge(w_high, n + 1)
                    low_part(dve, flat(split[:, 1, :, :]), raw, flat(split[:, 0, :, :])).then_inc(w_split, 1)

                def stats_1(at, b):
                    dve.wait_ge(x_loaded, 16 * (b + 1))
                    statistics(dve, x_in, ve, var1, CHAIN, at, link)

                def normalise_1(b):
                    dve.wait_ge(rstd1_done, b + 1)
                    normalise(dve, x_in, xn, xn_done)

                def row_max(at, tile):
                    later, n = tile
                    h, t = n // T, n % T
                    s = take(at, ("s", later, n))
                    dve.tensor_reduce(rowmax[:, h // HG, t, h % HG:h % HG + 1], s[:, 0:N + P * (t + 1)], AX.X,
                                      ALU.max, negate=True).then_inc(d_done, 1)
                    if n % (HG * T) == HG * T - 1:
                        g = h // HG
                        done(at, ("s", later, n))
                        link(at, ("mx", later, g), dve.tensor_copy(mx2[:, g, :, 0, :], rowmax[:, g, :, :]))
                        dve.tensor_tensor(mx2[:, g, :, 1, :], rowmax[:, g, :, :], mx2[:, g, :, 0, :],
                                          ALU.subtract).then_inc(max_split, 1)

                def normalise_heads(at, g):
                    s = take(at, ("oT", g))[:, 0:N].rearrange("p (t h c) -> p t h c", t=T, h=HG)
                    link(at, ("oT", g), dve.reciprocal(rinv[:, g, :, :], s[:, :, :, DH]))
                    dst = o_sb[:, :, HG * DH * g:HG * DH * (g + 1)].rearrange("p t (h c) -> p t h c", h=HG)
                    dve.tensor_tensor(dst, s[:, :, :, 0:DH],
                                      rinv[:, g, :, :].unsqueeze(3).broadcast_to([P, T, HG, DH]),
                                      ALU.mult).then_inc(d_done, 1)

                def low(at, key, split, signal, value):
                    s = take(at, key)
                    dve.wait_ge(signal, value)
                    low_part(dve, flat(split[:, 1, :, :]), s, flat(split[:, 0, :, :])).then_inc(d_done, 1)

                def front(at, key, b, after=None):
                    if key == ("xT",):
                        low(at, key, xnT, front_high, 2 * b + 1)
                    elif key == ("cT",):
                        low(at, key, cT, front_high, 2 * b + 2)
                    elif key[0] in ("q", "k"):
                        s, n = take(at, key), FRONT.index(key) - 2
                        dve.wait_ge(part1_done, 3 * b + n + 1)
                        if n > 0:
                            dve.wait_ge(parts_done, 3 * b + n)
                        dve.tensor_tensor(rest[:, :], s, parts[:, 0, n, :], ALU.subtract).then_inc(d_done, 1)
                        done(at, key)
                        dve.tensor_copy(parts[:, 1, n, :], rest[:, :]).then_inc(part2_done, 1)
                    else:
                        c = key[1]
                        s = take(at, key).rearrange("p (t h c) -> p t h c", t=T, h=H)
                        if after is not None:
                            dve.wait_ge(pv_done, after)
                        dve.tensor_copy(v_sb[:, T * c:T * (c + 1), :, 0:DH], s).then_inc(d_done, 1)

                def attention(at, more):
                    b = at[1]
                    for u in range(UNITS):
                        for tile in unit_tiles(u, more):
                            row_max(at, tile)
                        if u % JT == 1 and u > JT:
                            normalise_heads(at, u // JT - 1)
                        if more and u in FRONT_AT:
                            front(at, FRONT_AT[u], b + 1)
                        if more and u == STATS_AT:
                            stats_1(at, b + 1)
                        if more and u == NORM_AT:
                            normalise_1(b + 1)
                    if more:
                        front(at, ("v", 0), b + 1, after=UNITS * (b + 1))
                    normalise_heads(at, G - 1)
                    if more:
                        front(at, ("v", 1), b + 1)
                        for tile in tail_tiles(0):
                            row_max(at, tile)
                    low(at, ("dT",), oT, heads_high, b + 1)
                    if more:
                        for tile in tail_tiles(1):
                            row_max(at, tile)
                    dve.wait_ge(res_done, b + 1)
                    for c in range(2):
                        s = take(at, ("out", c)).rearrange("p (t d) -> p t d", d=D)[:, 0:2, :]
                        rows = res[:, 2 * c:2 * c + 2, :]
                        dve.tensor_tensor(rows, rows, s, ALU.add).then_inc(d_done, 1)

                at0 = ("before", 0)
                dve.memset(ps_o[:, :], 0.0).then_inc(dve_setup, 1)
                stats_1(at0, 0)
                normalise_1(0)
                weight_low(0)
                weight_low(1)
                for key in FRONT:
                    front(at0, key, 0)
                dve.wait_ge(const_loaded, 16 * 4)
                dve.wait_ge(ident_loaded, 16)
                dve.tensor_copy(identb[:, :], identf[:, :]).then_inc(dve_setup, 1)
                dve.tensor_copy(maskb[:, :], maskf).then_inc(dve_setup, 1)
                dve.wait_ge(raw_loaded, 16 * BR * 8)
                for name, raw, rem, p3 in (("b2", b2raw, b2rem, b2p), ("b1", b1raw, b1rem, b1p)):
                    link(at0, (name, 0), dve.tensor_copy(p3[0], raw))
                    link(at0, (name, 1), dve.tensor_tensor(rem, raw, p3[0], ALU.subtract))
                    link(at0, (name, 2), dve.tensor_copy(p3[1], rem))
                    last = dve.tensor_tensor(p3[2], rem, p3[1], ALU.subtract)
                    if name == "b2":
                        link(at0, (name, 3), last)
                last.then_inc(bias_split, 1)
                dve.wait_ge(node_high, 1)
                low_part(dve, node[:, 1, :, :].rearrange("p k n -> p (k n)"), ps_o[:, 0:KC * 96],
                         node[:, 0, :, :].rearrange("p k n -> p (k n)")).then_inc(node_done, 1)
                weight_low(2)
                weight_low(3)
                dve.tensor_scalar(mk[0:SK, :, :].rearrange("p t (a c) -> p (t a) c", a=2),
                                  path[:, :].unsqueeze(2).broadcast_to([SK, BR * LEAVES, LEAF_W]), BIG, None,
                                  ALU.mult).then_inc(dve_setup, 1)
                for k in range(PARTS):
                    last = dve.tensor_copy(ohm[0:SK, :, LEAVES * k:LEAVES * (k + 1)],
                                           path[:, :].rearrange("p (r l) -> p r l", r=BR))
                last.then_inc(dve_setup, 1)
                for n in range(LEAD):
                    row_max(at0, (0, n))
                weight_low(4)
                with dve.Fori(0, B - 1) as b:
                    attention(("batch", b), True)
                attention(("last", B - 1), False)

            @block.tensor
            def _(pe):
                def open_d(at, key, source=None):
                    RING_D.wait_free(pe, at, key, d_done, source)
                    return d_slot(at, key)

                def open_a(at, key):
                    RING_A.wait_free(pe, at, key, a_done)
                    return a_slot(at, key)

                def row_scores(at, tile):
                    later, n = tile
                    h, t = n // T, n % T
                    if n % (HG * T) == 0:
                        pe.wait_ge(stacked[h // HG], 16 * STACK * (at[1] + later + 1))
                    s = open_d(at, ("s", later, n))
                    q = qs[0:SK, h, tiles(t)]
                    pe.matmul(s[:, 0:N], q, ks[0:SK, h, 0:N], start=True, stop=True)
                    c = N + P * t
                    pe.matmul(s[:, N:c + P], q, ks[0:SK, h, N:c + P], start=True, stop=False)
                    pe.matmul(s[:, c:c + P], identb[:, :], maskb[:, :], start=False, stop=True).then_inc(d_full, 1)

                def turn_max(at, g, number):
                    pe.wait_ge(max_split, number)
                    s = open_a(at, ("m", g))[:, 0:N // 2].bitcast(BF16)
                    for t in range(T):
                        mm = pe.transpose(s[0:2 * HG, tiles(t)], mx2[:, g, t, :, :].rearrange("p k h -> p (k h)"),
                                          identb[:, :])
                    mm.then_inc(a_full, 1)

                def key_scores(at, u, heads):
                    if u % JT == 0 and heads[0] == 0:
                        pe.wait_ge(mrow_stacked, 32 * (G * at[1] + u // JT + 1))
                    u = u % UNITS
                    g, jt = u // JT, u % JT
                    c = first_column(jt)
                    for h in heads:
                        s = open_a(at, ("e", u, h))
                        pe.matmul(s[:, c:N], ks[0:SK + 2, HG * g + h, tiles(jt)], qs[0:SK + 2, HG * g + h, c:N],
                                  start=True, stop=True).then_inc(a_full, 1)

                def weigh(at, u):
                    g, jt = u // JT, u % JT
                    c = first_column(jt)
                    b = at[1]
                    if jt == 0 and g > 0:
                        pe.wait_ge(pv_copied, G * b + g)
                    if u == 0 and at[0] != "before":
                        pe.wait_ge(a_done, RING_A.per * b + len(RING_A.number["before"]))
                        pe.wait_ge(d_done, RING_D.per * b + len(RING_D.number["before"]))
                    elif jt < T:
                        pe.wait_ge(a_done, RING_A.count(at, ("e", u, HG - 1)))
                    else:
                        pe.wait_ge(masked, G * T * b + T * g + jt - T + 1)
                    for h in range(HG):
                        mm = pe.matmul(ps_o[32 * h:32 * h + VW, c:N], v_sb[:, jt, HG * g + h, :],
                                       probs[:, u % 3, h, c:N], start=(jt == 0), stop=(jt == JT - 1))
                    mm.then_inc(pv_done, 1)

                def turn_heads(at, g):
                    pe.wait_ge(pv_copied, G * at[1] + g + 1)
                    s = open_d(at, ("oT", g))
                    for t in range(T):
                        mm = pe.transpose(s[:, tiles(t)], pv_sb[:, tiles(t)], identf[:, :])
                    mm.then_inc(d_full, 1)

                def front(at, key, b):
                    if key == ("xT",):
                        pe.wait_ge(xn_done, b + 1)
                        mm = turn_rows(pe, open_d(at, key), xn)
                    elif key == ("cT",):
                        pe.wait_ge(ctx_loaded, 16 * (b + 1))
                        mm = turn_rows(pe, open_d(at, key), ctx_in)
                    elif key == ("q",):
                        if at[0] != "before":
                            pe.wait_ge(stacked[G - 1], 16 * STACK * b)
                        s = open_d(at, key, ("xT",))
                        for f in range(2):
                            mm = product(pe, s[:, N * f:N * (f + 1)],
                                         [(both(wq_sb, k, tiles(f)), both(xnT, k, slice(0, N))) for k in range(KC)])
                    elif key[0] == "k":
                        s, f = open_d(at, key, ("cT",)), key[1]
                        for c, src in enumerate((cT, xnT)):
                            mm = product(pe, s[:, N * c:N * (c + 1)],
                                         [(both(wkv_sb, k, tiles(f)), both(src, k, slice(0, N))) for k in range(KC)])
                    else:
                        s, src = open_d(at, key), (cT, xnT)[key[1]]
                        for t in range(T):
                            mm = product(pe, s[:, D * t:D * (t + 1)],
                                         [(both(src, k, tiles(t)), both(wkv_sb, k, slice(D, 2 * D)))
                                          for k in range(KC)])
                    mm.then_inc(d_full, 1)

                def attention(at, more):
                    b = at[1]
                    for u in range(UNITS):
                        tiles_here = unit_tiles(u, more)
                        for k in range(2):
                            if u + 1 < UNITS or more:
                                key_scores(at, u + 1, (2 * k, 2 * k + 1))
                            for tile in tiles_here[:1] if k == 0 else tiles_here[1:]:
                                row_scores(at, tile)
                        if u % JT == M_AT and (u // JT + 1 < G or more):
                            g = u // JT + 1
                            turn_max(at, g % G, G * b + g + 1)
                        if u % JT == 1 and u > JT:
                            turn_heads(at, u // JT - 1)
                        if more and u in FRONT_AT:
                            front(at, FRONT_AT[u], b + 1)
                        weigh(at, u)
                    if more:
                        front(at, ("v", 0), b + 1)
                    turn_heads(at, G - 1)
                    if more:
                        front(at, ("v", 1), b + 1)
                        for tile in tail_tiles(0):
                            row_scores(at, tile)
                    turn_rows(pe, open_d(at, ("dT",), ("oT", G - 1)), o_sb).then_inc(d_full, 1)
                    if more:
                        for tile in tail_tiles(1):
                            row_scores(at, tile)
                    for c in range(2):
                        s = open_d(at, ("out", c), ("dT",))
                        for k2 in range(2):
                            mm = product(pe, s[:, D * k2:D * (k2 + 1)],
                                         [(both(oT, k, tiles(2 * c + k2)), both(wout_sb, k, slice(0, D)))
                                          for k in range(KC)])
                        mm.then_inc(d_full, 1)

                at0 = ("before", 0)
                pe.wait_ge(ident_loaded, 16)
                front(at0, ("xT",), 0)
                front(at0, ("cT",), 0)
                pe.wait_ge(w_split, 1)
                front(at0, ("q",), 0)
                pe.wait_ge(w_split, 2)
                for key in FRONT[3:]:
                    front(at0, key, 0)
                pe.wait_ge(raw_loaded, 16 * BR * 8)
                pe.wait_ge(dve_setup, 1)
                for k in range(KC):
                    mm = pe.transpose(ps_o[:, 96 * k:96 * (k + 1)], noderaw[:, tiles(k)], identf[0:96, 0:96])
                mm.then_inc(node_turned, 1)
                pe.wait_ge(pool_setup, 7)
                pe.wait_ge(dve_setup, 3)
                for n in range(LEAD):
                    row_scores(at0, (0, n))
                turn_max(at0, 0, 1)
                pe.wait_ge(w_split, 5)
                pe.wait_ge(mrow_stacked, 32)
                for h in range(HG):
                    s = open_a(at0, ("e", 0, h))
                    pe.matmul(s, ks[0:SK + 2, h, tiles(0)], qs[0:SK + 2, h, :],
                              start=True, stop=True).then_inc(a_full, 1)
                pe.wait_ge(node_done, 1)
                pe.wait_ge(dve_setup, 5)
                pe.wait_ge(bias_rows, 16 * 2 * PARTS)
                with pe.Fori(0, B - 1) as b:
                    attention(("batch", b), True)
                attention(("last", B - 1), False)

        with ExitStack() as es:
            def sb2(name, shape, dt=F32):
                return es.enter_context(nc.sbuf_tensor(name, shape, dt))

            p2 = work[:, 0:2048].rearrange("p (t n) -> p t n", t=T)
            res = work[:, 2048:3072].rearrange("p (t d) -> p t d", t=T)
            x1n = work[:, 6144:7168].rearrange("p (t d) -> p t d", t=T)
            w1 = [w1q] + [sb2(f"w1{r}", [P, 2, KC, HID], F32R) for r in "kv"]
            w2 = [w2q] + [sb2(f"w2{r}", [P, 2, HT, D], F32R) for r in "kv"]
            splits = [w1[1], w2[1], w1[2], w2[2]]
            y_sb = sb2("y_sb", [P, T, D])
            yT = sb2("yT", [P, 2, KC, N], F32R)
            hidden = sb2("hidden", [P, 2, HT, N], F32R)
            p2T = hidden
            qk2T = [sb2(f"{r}2T", [P, 2, KC, N], F32R) for r in "qk"]
            v2 = sb2("v2", [P, 2, T, D], F32R)
            onehot = sb2("onehot", [48, BR, N], BF16)
            g0 = sb2("g0", [96, N], BF16)
            carrier_m = sb2("carrier_m", [P, 1])
            nmax, nmaxs = sb2("nmax", [P, T]), sb2("nmaxs", [P, T])
            sums, rs2 = sb2("sums", [P, T]), sb2("rs2", [P, T])

            def h_slot(at, key):
                return ps_a[:, RING_H.slot(at, key), :]

            def f_slot(at, key):
                return ps_d[:, RING_F.slot(at, key), :]

            block = es.enter_context(nc.Block())

            @block.sync
            def _(sp):
                def load(dst, src, signal):
                    sp.dma_start(dst, src).then_inc(signal, 16)

                load(x1n, rows_of(x1_dram, 0), x1_loaded)
                sp.wait_ge(w2_split, 1)
                load(raw2[3].rearrange("p (t d) -> p t d", t=HT),
                     ffn[2][4].rearrange("(t a) h d -> (a h) t d", a=2), last_loaded)

                def store(at):
                    sp.wait_ge(f_done, RING_F.count(at, ("y", 1)))
                    load(rows_of(out, at[1]), res, stored)

                with sp.Fori(0, B - 1) as b:
                    sp.wait_ge(x1_moved, b + 1)
                    sp.wait_ge(yn_done, b + 1)
                    load(x1n, rows_of(x1_dram, b + 1), x1_loaded)
                    store(("batch", b))
                store(("last", B - 1))
                sp.wait_ge(stored, 16 * B)

            @block.gpsimd
            def _(pool):
                def rstd_2(b):
                    pool.wait_ge(var2, b + 1)
                    pool.tensor_tensor(rstd[:, :], ve[:, :], half[:, :], ALU.pow).then_inc(rstd2_done, 1)

                def move(b, stores=None):
                    if stores is not None:
                        pool.wait_ge(stored, stores)
                    pool.wait_ge(x1_loaded, 16 * (b + 1))
                    pool.tensor_tensor(carrier_m[:, :], half[:, 0:1], half[:, 0:1], ALU.add)
                    pool.tensor_copy(res, x1n).then_inc(x1_moved, 1)

                rstd_2(0)
                pool.wait_ge(w2_split, 2)
                move(0)
                with pool.Fori(0, B - 1) as b:
                    rstd_2(b + 1)
                    move(b + 1, stores=16 * (b + 1))

            @block.scalar
            def _(act):
                def high(at, key, dst, func=ACT.Copy):
                    act.wait_ge(h_full, RING_H.count(at, key))
                    act.activation(dst, h_slot(at, key), func).then_inc(h_high, 1)

                def branch_high(at, r, dst):
                    act.wait_ge(f_full, RING_F.count(at, ("f", r)))
                    act.activation(dst, f_slot(at, ("f", r)), ACT.Copy).then_inc(f_high, 1)

                def weight_high(n):
                    if n < 3:
                        act.wait_ge(raw2_loaded, 16 * 5)
                    else:
                        act.wait_ge(last_loaded, 16)
                    act.activation(flat(splits[n][:, 0, :, :]), raw2[n], ACT.Copy).then_inc(w2_high, 1)

                def feedforward(at, more):
                    b = at[1]
                    for r in range(BR):
                        for t in range(HT):
                            high(at, ("h", r, t), hidden[:, 0, t, :], ACT.Relu)
                        if r < 2:
                            branch_high(at, r, flat(qk2T[r][:, 0, :, :]))
                    if more:
                        for k in range(KC):
                            high(at, ("yT", k), yT[:, 0, k, :])
                    for t in range(T):
                        act.wait_ge(x_max, T * b + t + 1)
                        act.activation(p2[:, t, :], ps_o[:, :], ACT.Exp, bias=nmaxs[:, t:t + 1], scale=SCALE2,
                                       accum_out=sums[:, t:t + 1]).then_inc(x_done, 1)
                    branch_high(at, 2, flat(v2[:, 0, :, :]))
                    for t in range(T):
                        high(at, ("pT", t), p2T[:, 0, t, :])

                for n in range(3):
                    weight_high(n)
                for k in range(KC):
                    high(("before", 0), ("yT", k), yT[:, 0, k, :])
                weight_high(3)
                with act.Fori(0, B - 1) as b:
                    feedforward(("batch", b), True)
                feedforward(("last", B - 1), False)

            @block.vector
            def _(dve):
                def link(at, key, ins):
                    ins.then_inc(chain2, 1)
                    dve.wait_ge(chain2, CHAIN2.count(at, key))

                def take(at, key):
                    dve.wait_ge(f_full, RING_F.count(at, key))
                    return f_slot(at, key)

                def low(at, key, dst, high):
                    dve.wait_ge(h_high, HIGH_H.count(at, key))
                    low_part(dve, dst, h_slot(at, key), high).then_inc(h_done, 1)

                def branch_low(at, r, split):
                    dve.wait_ge(f_high, BR * at[1] + r + 1)
                    low_part(dve, flat(split[:, 1, :, :]), f_slot(at, ("f", r)),
                             flat(split[:, 0, :, :])).then_inc(f_done, 1)

                def weight_low(n):
                    dve.wait_ge(w2_high, n + 1)
                    low_part(dve, flat(splits[n][:, 1, :, :]), raw2[n], flat(splits[n][:, 0, :, :])).then_inc(w2_split, 1)

                def stats_2(at, b):
                    dve.wait_ge(x1_loaded, 16 * (b + 1))
                    statistics(dve, x1n, ve, var2, CHAIN2, at, link)

                def normalise_2(b):
                    dve.wait_ge(rstd2_done, b + 1)
                    normalise(dve, x1n, y_sb, yn_done)

                def decisions(at, b):
                    s = take(at, ("node",))[:, :]
                    dve.tensor_scalar(g0[:, :], s[0:96, 0:N], nb[:, 0:1], 0.0, ALU.add, ALU.is_ge).then_inc(f_done, 1)
                    dve.wait_ge(f_done, RING_F.count(at, ("node",)))
                    dve.tensor_scalar(gates[0:96, :], g0[:, :], flip[:, 0:1], None,
                                      ALU.not_equal).then_inc(gates_done, 1)

                def chosen_leaves(at):
                    for r in range(BR):
                        dve.wait_ge(h_full, RING_H.count(at, ("one", r)))
                        dve.tensor_scalar(onehot[:, r, :], h_slot(at, ("one", r))[0:48], 0.0, None,
                                          ALU.max).then_inc(h_done, 1)

                def feedforward(at, more):
                    b = at[1]
                    for r in range(BR):
                        for t in range(HT):
                            key = ("h", r, t)
                            dve.wait_ge(h_high, HIGH_H.count(at, key))
                            dve.scalar_tensor_tensor(out=hidden[:, 1, t, :], in0=h_slot(at, key), scalar=0.0,
                                                     in1=hidden[:, 0, t, :].bitcast(F32), op0=ALU.max,
                                                     op1=ALU.subtract).then_inc(h_done, 1)
                        if r == 1 and more:
                            stats_2(at, b + 1)
                            normalise_2(b + 1)
                        if r < 2:
                            branch_low(at, r, qk2T[r])
                    if more:
                        for k in range(KC):
                            low(at, ("yT", k), yT[:, 1, k, :], yT[:, 0, k, :])
                    for t in range(T):
                        dve.wait_ge(x_full, T * b + t + 1)
                        link(at, ("x", t), dve.tensor_reduce(nmax[:, t:t + 1], ps_o[:, :], AX.X, ALU.max,
                                                             negate=True))
                        dve.tensor_scalar(nmaxs[:, t:t + 1], nmax[:, t:t + 1], SCALE2, None,
                                          ALU.mult).then_inc(x_max, 1)
                    branch_low(at, 2, v2)
                    for t in range(T):
                        if t == 2 and more:
                            decisions(at, b + 1)
                        low(at, ("pT", t), p2T[:, 1, t, :], p2T[:, 0, t, :])
                    dve.wait_ge(x_done, T * b + T)
                    link(at, ("sum",), dve.reciprocal(rs2[:, :], sums[:, :]))
                    dve.wait_ge(x1_moved, b + 1)
                    for c in range(2):
                        s = take(at, ("y", c)).rearrange("p (t d) -> p t d", d=D)
                        for k in range(2):
                            t = 2 * c + k
                            last = dve.scalar_tensor_tensor(out=res[:, t, :], in0=s[:, k, :],
                                                            scalar=rs2[:, t:t + 1], in1=res[:, t, :],
                                                            op0=ALU.mult, op1=ALU.add)
                        last.then_inc(f_done, 1)
                        if c == 0 and more:
                            chosen_leaves(at)

                at0 = ("before", 0)
                stats_2(at0, 0)
                weight_low(0)
                normalise_2(0)
                weight_low(1)
                for k in range(KC):
                    low(at0, ("yT", k), yT[:, 1, k, :], yT[:, 0, k, :])
                decisions(at0, 0)
                chosen_leaves(at0)
                weight_low(2)
                weight_low(3)
                with dve.Fori(0, B - 1) as b:
                    feedforward(("batch", b), True)
                feedforward(("last", B - 1), False)

            @block.tensor
            def _(pe):
                def open_f(at, key, source=None):
                    RING_F.wait_free(pe, at, key, f_done, source)
                    return f_slot(at, key)

                def open_h(at, key):
                    RING_H.wait_free(pe, at, key, h_done)
                    return h_slot(at, key)

                def turned(at, b):
                    pe.wait_ge(yn_done, b + 1)
                    for k in range(KC):
                        s = open_h(at, ("yT", k))
                        for t in range(T):
                            mm = pe.transpose(s[:, tiles(t)], y_sb[:, t, tiles(k)], identf[:, :])
                        mm.then_inc(h_full, 1)

                def decide(at):
                    pe.wait_ge(h_done, RING_H.count(at, TURN_Y[-1]))
                    s = open_f(at, ("node",))
                    product(pe, s[0:96, 0:N], [(both(node, k, slice(0, 96)), both(yT, k, slice(0, N)))
                                               for k in range(KC)]).then_inc(f_full, 1)

                def choose_leaves(at, b):
                    pe.wait_ge(gates_done, b + 1)
                    for r in range(BR):
                        s = open_h(at, ("one", r))
                        pe.matmul(s[0:48, :], ohm[:, r, :], gates[:, :], start=True, stop=True).then_inc(h_full, 1)

                def hidden_layer(at, r):
                    for t in range(HT):
                        s = open_h(at, ("h", r, t))
                        product(pe, s, [(both(w1[r], k, tiles(t)), both(yT, k, slice(0, N))) for k in range(KC)],
                                last=False)
                        pe.matmul(s, mk[:, HT * r + t, :], gates[:, :], start=False, stop=True).then_inc(h_full, 1)

                def feedforward(at, more):
                    b = at[1]
                    for r in range(2):
                        if r > 0:
                            pe.wait_ge(w2_split, 2)
                        hidden_layer(at, r)
                        s = open_f(at, ("f", r))
                        for t in range(HT):
                            pe.wait_ge(h_done, RING_H.count(at, ("h", r, t)))
                            for k in range(KC):
                                product(pe, s[:, N * k:N * (k + 1)],
                                        [(both(w2[r], t, tiles(k)), both(hidden, t, slice(0, N)))],
                                        first=(t == 0), last=False)
                        for k in range(KC):
                            mm = pe.matmul(s[:, N * k:N * (k + 1)], b2s[:, r, tiles(k)], onehot[:, r, :],
                                           start=False, stop=True)
                        mm.then_inc(f_full, 1)
                    pe.wait_ge(w2_split, 4)
                    hidden_layer(at, 2)
                    if more:
                        turned(at, b + 1)
                    pe.wait_ge(f_done, RING_F.count(at, ("f", 1)))
                    for t in range(T):
                        if t > 0:
                            pe.wait_ge(x_done, T * b + t)
                        product(pe, ps_o[:, :], [(both(qk2T[0], k, tiles(t)), both(qk2T[1], k, slice(0, N)))
                                                 for k in range(KC)]).then_inc(x_full, 1)
                        if t == 0:
                            v = open_f(at, ("f", 2))
                            pe.wait_ge(h_done, RING_H.count(at, ("h", 2, HT - 1)))
                        s = v[:, D * t:D * (t + 1)]
                        product(pe, s, [(both(hidden, j, tiles(t)), both(w2[2], j, slice(0, D))) for j in range(HT)],
                                last=False)
                        mm = pe.matmul(s, onehot[:, 2, tiles(t)], b2s[:, 2, :], start=False, stop=True)
                    mm.then_inc(f_full, 1)
                    for t in range(T):
                        if t == T - 1 and more:
                            decide(at)
                        s = open_h(at, ("pT", t))
                        pe.wait_ge(x_done, T * b + t + 1)
                        for j in range(T):
                            mm = pe.transpose(s[:, tiles(j)], p2[:, t, tiles(j)], identf[:, :])
                        mm.then_inc(h_full, 1)
                    pe.wait_ge(f_done, RING_F.count(at, ("f", 2)))
                    for c in range(2):
                        s = open_f(at, ("y", c))
                        for k in range(2):
                            t = 2 * c + k
                            pe.wait_ge(h_done, RING_H.count(at, ("pT", t)))
                            mm = product(pe, s[:, D * k:D * (k + 1)],
                                         [(both(p2T, t, tiles(j)), both(v2, j, slice(0, D))) for j in range(T)])
                        mm.then_inc(f_full, 1)
                        if c == 0 and more:
                            choose_leaves(at, b + 1)

                at0 = ("before", 0)
                turned(at0, 0)
                decide(at0)
                choose_leaves(at0, 0)
                with pe.Fori(0, B - 1) as b:
                    feedforward(("batch", b), True)
                feedforward(("last", B - 1), False)


def constants():
    import numpy as np

    ident = np.eye(P, dtype=np.float32)
    mask = np.where(np.arange(P)[None, :] > np.arange(P)[:, None], np.float32(-BIG), np.float32(0))
    path = np.zeros((96, BR * LEAVES), np.float32)
    flip = np.zeros((96, 1), np.float32)
    for r in range(BR):
        flip[32 * r + NODES:32 * r + 2 * NODES] = 1
        for leaf in range(LEAVES):
            node = leaf + NODES
            while node:
                right, node = (node - 1) % 2, (node - 1) // 2
                path[32 * r + node + (NODES if right else 0), r * LEAVES + leaf] = -1
    return {"c_ident": ident, "c_mask": mask.astype(np.float32), "c_path": path, "c_flip": flip}


_FFN = ["node_w", "node_b", "w1", "b1", "w2", "b2"]
_INS = (["x", "ctx_1024", "L0_xattn_Wq", "L0_xattn_Wkv", "L0_xattn_Wout", "L0_xattn_bout"]
        + [f"L0_ffn_{r}_{n}" for r in "qkv" for n in _FFN])


def by_column(w):
    return w.reshape(D, G, HG, DH).transpose(0, 1, 3, 2).reshape(D, D)


def kernel(**inputs):
    import numpy as _np
    import concourse.bacc as _bacc
    from concourse import mybir as _mybir
    from concourse.bass_utils import run_bass_kernel_spmd as _run

    nc = _bacc.Bacc("TRN2", target_bir_lowering=False, num_devices=1)
    arrays, args = {}, []
    consts = constants()
    for name in _INS + list(consts):
        a = _np.asarray(inputs[name] if name in inputs else consts[name])
        if name == "L0_xattn_Wq":
            a = by_column(a)
        if name == "L0_xattn_Wkv":
            a = _np.concatenate([by_column(a[:, :D]), a[:, D:]], axis=1)
        a = _np.ascontiguousarray(a)
        arrays[f"in_{name}_dram"] = a
        args.append(nc.dram_tensor(f"in_{name}_dram", a.shape, _mybir.dt.from_np(a.dtype), kind="ExternalInput").ap())
    out = nc.dram_tensor("out_0_dram", (B, N, D), _mybir.dt.float32, kind="ExternalOutput").ap()
    ffn = [args[6 + 6 * r:12 + 6 * r] for r in range(BR)]
    program(nc, *args[:6], ffn, *args[24:28], out)
    r = _run(nc, [arrays], core_ids=[0])
    return r.results[0]["out_0_dram"]
```

```python
from contextlib import ExitStack

import concourse.bass as bass
from concourse import mybir

F32 = mybir.dt.float32
F32R = mybir.dt.float32r
BF16 = mybir.dt.bfloat16
ALU = mybir.AluOpType
ACT = mybir.ActivationFunctionType
AX = mybir.AxisListType

P = 128
B, N, D = 8, 512, 256
H = 16
DH = D // H
HG = 4
G = H // HG
T = N // P
KC = D // P
J = 2 * N
JT = J // P
LEAVES, LEAF_W, NODES = 16, 64, 15
BR = 3
HID = LEAVES * LEAF_W
HT = HID // P
PARTS = 3
PAIRS = ((0, 0), (0, 1), (1, 0), (1, 1), (0, 2), (2, 0))
SK = len(PAIRS) * DH
VW = DH + 1
BIG = 1e30
EPS = 1e-5
SCALE1 = float(DH) ** -0.5
SCALE2 = float(D) ** -0.5

UNITS = G * JT
STILES = H * T
LEAD = 28
S_PER_UNIT = (3, 2, 2, 2, 2, 2, 1, 1)
TAIL = STILES - G * sum(S_PER_UNIT)
STACK = 2 * len(PAIRS)
M_AT = 4

FRONT = [("cT",), ("xT",), ("q",), ("k", 0), ("k", 1)]
V_TILES = ((0, 1), (2, 3), (4,), (5,), (6,), (7,))
FRONT_AT = {6: ("cT",), 7: ("xT",), 8: ("q",), 9: ("k", 0), 11: ("k", 1)}
THIRD_AT = (9, 10, 15)
STATS_AT, NORM_AT = 2, 5


def row_tiles(n, count, more):
    tiles = [divmod(m, STILES) for m in range(n, n + count)]
    return [(k, m) for k, m in tiles if k == 0 or more]


def unit_tiles(u, more):
    return row_tiles(LEAD + sum(S_PER_UNIT) * (u // JT) + sum(S_PER_UNIT[:u % JT]), S_PER_UNIT[u % JT], more)


def tail_tile(part):
    return divmod(STILES + LEAD - TAIL + part, STILES)


def uses_d(more):
    keys = []
    for u in range(UNITS):
        s = [("s",) + n for n in unit_tiles(u, more)]
        keys += s[:1]
        if u % JT == 1 and u > JT:
            keys += [("oT", u // JT - 1)]
        keys += s[1:]
        if more and u in FRONT_AT:
            keys += [FRONT_AT[u]]
    if not more:
        return keys + [("oT", G - 1), ("dT",), ("out", 0), ("out", 1)]
    s = [("s",) + tail_tile(n) for n in range(TAIL)]
    return keys + [("oT", G - 1)] + s[:2] + [("dT",)] + s[2:] + [("out", 0), ("out", 1)]


V_KEYS = [("v", n) for n in range(len(V_TILES))]


def uses_a(more):
    keys = []
    for u in range(UNITS):
        if u + 1 < UNITS or more:
            keys += [("e", (u + 1) % UNITS, h) for h in range(HG)]
        if u % JT == M_AT and (u // JT + 1 < G or more):
            keys += [("m", (u // JT + 1) % G)]
    return keys + (V_KEYS if more else [])


def chain_steps(where):
    def mx(n):
        return [("mx", n[0], n[1] // (HG * T))] if n[1] % (HG * T) == HG * T - 1 else []

    if where == "before":
        steps = [("ln", 0), ("ln", 1)]
        steps += [("b2", 0), ("b2", 1), ("b2", 2), ("b2", 3), ("b1", 0), ("b1", 1), ("b1", 2)]
        for n in range(LEAD):
            steps += mx((0, n))
        return steps
    more, steps = where == "batch", []
    for u in range(UNITS):
        here = unit_tiles(u, more)
        for n in here[:1]:
            steps += mx(n)
        if u % JT == 1 and u > JT:
            steps += [("oT", u // JT - 1)]
        for n in here[1:]:
            steps += mx(n)
        if more and u == STATS_AT:
            steps += [("ln", 0), ("ln", 1)]
    steps += [("oT", G - 1)]
    if more:
        for n in range(TAIL):
            steps += mx(tail_tile(n))
    else:
        steps.insert(steps.index(("oT", 2)) + 1, ("ln2", 0))
        steps.insert(steps.index(("ln2", 0)) + 1, ("ln2", 1))
    return steps


class Order:

    def __init__(self, before, batch, last):
        self.per, first = len(batch), len(before)
        self.number = {"before": {key: n for n, key in enumerate(before)},
                       "batch": {key: first + n for n, key in enumerate(batch)},
                       "last": {key: first + n for n, key in enumerate(last)}}
        for where, keys in (("before", before), ("batch", batch), ("last", last)):
            assert len(self.number[where]) == len(keys), where

    def count(self, at, key):
        return at[1] * self.per + self.number[at[0]][key] + 1


class Ring(Order):

    def __init__(self, slots, *uses):
        super().__init__(*uses)
        self.slots = slots
        assert self.per % slots == 0, self.per

    def slot(self, at, key):
        return self.number[at[0]][key] % self.slots

    def wait_free(self, engine, at, key, emptied, source=None):
        number = self.number[at[0]]
        if source is not None and number[source] > number[key] - self.slots:
            engine.wait_ge(emptied, self.count(at, source))
        elif number[key] >= self.slots:
            engine.wait_ge(emptied, self.count(at, key) - self.slots)


RING_D = Ring(2, FRONT + [("s", 0, n) for n in range(LEAD)], uses_d(True), uses_d(False))
RING_A = Ring(3, V_KEYS + [("m", 0)] + [("e", 0, h) for h in range(HG)], uses_a(True), uses_a(False))
CHAIN = Order(*(chain_steps(where) for where in ("before", "batch", "last")))

TURN_Y = [("yT", k) for k in range(KC)]
ONES = [("one", r) for r in range(BR)]


def uses_h(more):
    return ([("h", r, t) for r in range(BR) for t in range(HT)] + (TURN_Y if more else [])
            + [("pT", t) for t in range(T)] + (ONES if more else []))


def uses_f(more):
    return [("f", r) for r in range(BR)] + ([("node",)] if more else []) + [("y", 0), ("y", 1)]


def highs(uses):
    return [key for key in uses if key[0] in ("h", "yT", "pT")]


RING_H = Ring(3, TURN_Y + ONES, uses_h(True), uses_h(False))
HIGH_H = Order(*(highs(uses) for uses in (TURN_Y, uses_h(True), uses_h(False))))
RING_F = Ring(2, [("node",)], uses_f(True), uses_f(False))


def links_2(more):
    ln = [("ln", 0), ("ln", 1)]
    return (ln if more else []) + [("x", t) for t in range(T)] + [("sum",)]


CHAIN2 = Order([], links_2(True), links_2(False))


def program(nc, x, ctx, wq, wkv, wout, bout, ffn, c_ident, c_mask, c_path, c_flip, out):
    keep = ExitStack()
    with keep:
        def sem(name):
            return keep.enter_context(nc.semaphore(name))

        def sb(name, shape, dt=F32):
            return keep.enter_context(nc.sbuf_tensor(name, shape, dt))

        x1_dram = nc.dram_tensor("x1_dram", (B, N, D), F32, kind="Internal").ap()

        w1q = sb("w1q", [P, 2, KC, HID], F32R)
        w2q = sb("w2q", [P, 2, HT, D], F32R)
        mk = sb("mk", [P, BR * HT, P], BF16)
        ohm = sb("ohm", [P, BR, 48], BF16)
        b2s = sb("b2s", [48, BR, D], BF16)
        node = sb("node", [P, 2, KC, 96], F32R)
        identf = sb("identf", [P, P])
        flip = sb("flip", [96, 1])
        nb = sb("nb", [96, 1])
        gates = sb("gates", [P, N], BF16)
        half = sb("half", [P, T])
        carrier_v = sb("carrier_v", [P, 1])
        st, mv = sb("st", [P, T, 6]), sb("mv", [P, T, 2])
        ve, rstd = sb("ve", [P, T]), sb("rstd", [P, T])
        work = sb("work", [P, 7 * T * D])
        x1n = work[:, 6144:7168].rearrange("p (t d) -> p t d", t=T)
        raw2 = [work[:, 2048 * n:2048 * (n + 1)] for n in (0, 1, 2, 0)]

        ps_d = keep.enter_context(nc.psum_tensor("ps_d", [P, 2, 1024], F32))
        ps_a = keep.enter_context(nc.psum_tensor("ps_a", [P, 3, 512], F32))
        ps_o = keep.enter_context(nc.psum_tensor("ps_o", [P, 512], F32))

        d_full, d_done = sem("d_full"), sem("d_done")
        a_full, a_done = sem("a_full"), sem("a_done")
        h_full, h_done = sem("h_full"), sem("h_done")
        f_full, f_done = sem("f_full"), sem("f_done")
        h_high, f_high = sem("h_high"), sem("f_high")
        x_loaded, ctx_loaded = sem("x_loaded"), sem("ctx_loaded")
        wq_loaded, wkv_loaded, wout_loaded = sem("wq_loaded"), sem("wkv_loaded"), sem("wout_loaded")
        w1q_loaded, w2q_loaded = sem("w1q_loaded"), sem("w2q_loaded")
        ident_loaded, const_loaded, raw_loaded = sem("ident_loaded"), sem("const_loaded"), sem("raw_loaded")
        raw_zeroed, pool_setup, dve_setup = sem("raw_zeroed"), sem("pool_setup"), sem("dve_setup")
        ones_set = sem("ones_set")
        w_high, w_split = sem("w_high"), sem("w_split")
        bias_split, bias_rows = sem("bias_split"), sem("bias_rows")
        node_turned, node_high, node_done = sem("node_turned"), sem("node_high"), sem("node_done")
        var1, rstd1_done, xn_done = sem("var1"), sem("rstd1_done"), sem("xn_done")
        residual_loaded, res_done = sem("residual_loaded"), sem("res_done")
        c_high, x_high, heads_high = sem("c_high"), sem("x_high"), sem("heads_high")
        part1_done, part2_done, parts_done = sem("part1_done"), sem("part2_done"), sem("parts_done")
        stacked = [sem(f"stacked{g}") for g in range(G)]
        max_split, mrow_stacked = sem("max_split"), sem("mrow_stacked")
        masked, pv_done, pv_copied = sem("masked"), sem("pv_done"), sem("pv_copied")
        x1_stored = sem("x1_stored")
        chain, chain2 = sem("chain"), sem("chain2")
        raw2_loaded, w2_high, w2_split = sem("raw2_loaded"), sem("w2_high"), sem("w2_split")
        w2_last_high = sem("w2_last_high")
        last_loaded = sem("last_loaded")
        x_full, x_max, x_done = sem("x_full"), sem("x_max"), sem("x_done")
        x1_loaded, res_loaded = sem("x1_loaded"), sem("res_loaded")
        var2, rstd2_done, yn_done, gates_done = sem("var2"), sem("rstd2_done"), sem("yn_done"), sem("gates_done")
        stored = sem("stored")

        def first_column(jt):
            return 0 if jt < T else P * (jt - T)

        def rows_of(array, b):
            return array[bass.ds(b, 1)].rearrange("o (t p) d -> p (o t) d", p=P)

        def tiles(t):
            return slice(P * t, P * (t + 1))

        def flat(array):
            return array.rearrange("p a b -> p (a b)")

        def both(array, *index):
            return tuple(array[(slice(None), part) + index] for part in (0, 1))

        def product(pe, dst, pairs, first=True, last=True):
            passes = [(w[i], m[j]) for w, m in pairs for i, j in ((1, 0), (0, 1), (0, 0))]
            for n, (w, m) in enumerate(passes):
                mm = pe.matmul(dst, w, m, start=first and n == 0, stop=last and n == len(passes) - 1)
            return mm

        def turn_rows(pe, dst, src):
            for k in range(KC):
                for t in range(T):
                    mm = pe.transpose(dst[:, N * k + P * t:N * k + P * (t + 1)], src[:, t, tiles(k)], identf[:, :])
            return mm

        def load_w1(queue, dst, r, signal):
            for k in range(KC):
                queue.dma_start(dst[:, HID * k:HID * (k + 1)].rearrange("p (l h) -> p l h", l=LEAVES),
                                ffn[r][2][:, P * k:P * (k + 1), :].rearrange("l p h -> p l h")).then_inc(signal, 16)

        def load_w2(queue, dst, r, signal):
            queue.dma_start(dst.rearrange("p (t d) -> p t d", t=HT),
                            ffn[r][4].rearrange("(t a) h d -> (a h) t d", a=2)).then_inc(signal, 16)

        def load_square(queue, dst, src, signal):
            queue.dma_start(dst.rearrange("p (k n) -> p k n", k=KC),
                            src.rearrange("(k p) n -> p k n", p=P)).then_inc(signal, 16)

        def low_part(dve, low, src, high):
            return dve.tensor_tensor(low, src, high.bitcast(F32), ALU.subtract)

        def statistics(dve, src, var, signal, at, link, name="ln"):
            for t in range(T):
                last = dve.bn_stats(st[:, t, :], src[:, t, :])
            link(at, (name, 0), last)
            dve.memset(carrier_v[:, 0:1], 0.0)
            for t in range(T):
                last = dve.bn_aggr(mv[:, t, :], st[:, t, :])
            link(at, (name, 1), last)
            dve.tensor_scalar(var[:, :], mv[:, :, 1], EPS, None, ALU.add).then_inc(signal, 1)

        def normalise(dve, src, dst, signal):
            for t in range(T):
                last = dve.tensor_scalar(dst[:, t, :], src[:, t, :], mv[:, t, 0:1], rstd[:, t:t + 1],
                                         ALU.subtract, ALU.mult)
            last.then_inc(signal, 1)

        with ExitStack() as es:
            def sb1(name, shape, dt=F32):
                return es.enter_context(nc.sbuf_tensor(name, shape, dt))

            parts = work[:, 0:4608].bitcast(BF16).rearrange("p (c s n) -> p c s n", c=PARTS, s=3)
            x_in = work[:, 4608:5632].rearrange("p (t d) -> p t d", t=T)
            xn = work[:, 5632:6656].rearrange("p (t d) -> p t d", t=T)
            ctx_in = sb1("ctx_in", [P, T, D])
            res = sb1("res", [P, T, D])
            xnT = sb1("xnT", [P, 2, KC, N], F32R)
            cT = sb1("cT", [P, 2, KC, N], F32R)
            oT = cT
            o_sb = sb1("o_sb", [P, T, D])
            pv_sb = sb1("pv_sb", [P, N])
            rest = sb1("rest", [P, J])
            qs = sb1("qs", [P, H, N], BF16)
            ks = sb1("ks", [P, H, J], BF16)
            v_sb = sb1("v_sb", [P, JT, H, VW])
            shared = sb1("shared", [P, 3 * HG * N])
            probs = shared[:, :].rearrange("p (s h n) -> p s h n", s=3, h=HG)
            wq_sb = sb1("wq_sb", [P, 2, KC, D], F32R)
            wkv_sb = sb1("wkv_sb", [P, 2, KC, 2 * D], F32R)
            wout_sb = sb1("wout_sb", [P, 2, KC, D], F32R)
            identb = sb1("identb", [P, P], BF16)
            maskb = sb1("maskb", [P, P], BF16)
            bias = sb1("bias", [P, D])
            path = sb1("path", [96, BR * LEAVES])
            rowmax = sb1("rowmax", [P, G, T, HG])
            mx2 = sb1("mx2", [P, G, T, 2, HG], BF16)
            mrow = sb1("mrow", [2 * HG, N], BF16)
            rinv = sb1("rinv", [P, G, T, HG])
            carrier_p = sb1("carrier_p", [P, UNITS])
            raw_q, raw_kv, raw_out, raw_ffn = (shared[:, 0:512], shared[:, 512:1536], shared[:, 1536:2048],
                                               shared[:, 2048:4096])
            b2raw = shared[0:48, 4096:4864].rearrange("p (r d) -> p r d", r=BR)
            b2rem = shared[0:48, 4864:5632].rearrange("p (r d) -> p r d", r=BR)
            o_flat = flat(o_sb[:, :, :])
            b2p = [area.bitcast(BF16).rearrange("p (r d) -> p r d", r=BR)
                   for area in (shared[0:48, 5632:6016], o_flat[0:48, 256:640], o_flat[0:48, 640:1024])]
            maskf = shared[:, 6016:6144]
            noderaw = o_flat[0:96, 0:D]
            b1raw, b1rem = pv_sb[0:BR * HT, 0:P], pv_sb[0:BR * HT, P:2 * P]
            b1p = [pv_sb[0:BR * HT, 256 + 64 * k:320 + 64 * k].bitcast(BF16) for k in range(PARTS)]
            weights = [(raw_q, wq_sb, wq_loaded), (raw_kv, wkv_sb, wkv_loaded), (raw_out, wout_sb, wout_loaded),
                       (raw_ffn, w1q, w1q_loaded), (raw_ffn, w2q, w2q_loaded)]

            def d_slot(at, key):
                return ps_d[:, RING_D.slot(at, key), :]

            def a_slot(at, key):
                return ps_a[:, RING_A.slot(at, key), :]

            block = es.enter_context(nc.Block())

            @block.sync
            def _(sp):
                def load(dst, src, signal):
                    sp.dma_start(dst, src).then_inc(signal, 16)

                load(x_in, rows_of(x, 0), x_loaded)
                load(identf[:, :], c_ident, ident_loaded)
                load(ctx_in[:, :, :], rows_of(ctx, 0), ctx_loaded)
                load(maskf, c_mask, const_loaded)
                load(path[:, :], c_path, const_loaded)
                load(flip[:, :], c_flip, const_loaded)
                load(bias[:, :], bout.partition_broadcast(P), const_loaded)
                sp.wait_ge(raw_zeroed, 2)
                for r in range(BR):
                    node_w, node_b, w1_d, b1_d, w2_d, b2_d = ffn[r]
                    for copy in range(2):
                        at = 32 * r + NODES * copy
                        load(noderaw[at:at + NODES, :], node_w, raw_loaded)
                        load(nb[at:at + NODES, :], node_b.rearrange("(n o) -> n o", o=1), raw_loaded)
                    load(b1raw[HT * r:HT * (r + 1), :], b1_d.rearrange("(t a) h -> t (a h)", a=2), raw_loaded)
                    for k in range(PARTS):
                        load(b2raw[LEAVES * k:LEAVES * (k + 1), r, :], b2_d, raw_loaded)

                def stack(g, sides="qk"):
                    rows = slice(HG * DH * (g % 2), HG * DH * (g % 2 + 1))
                    heads = slice(HG * g, HG * (g + 1))
                    for n, (qp, kp) in enumerate(PAIRS):
                        terms = slice(DH * n, DH * (n + 1))
                        f = g // 2
                        if "q" in sides:
                            load(qs[terms, heads, :], parts[rows, qp, 0, N * f:N * (f + 1)], stacked[g])
                        if "k" in sides:
                            load(ks[terms, heads, :], parts[rows, kp, 1 + f, :], stacked[g])

                def max_rows(at, g):
                    sp.wait_ge(a_done, RING_A.count(at, ("m", g)))
                    for k in range(2):
                        load(qs[SK + k:SK + k + 1, HG * g:HG * (g + 1), :],
                             mrow[HG * k:HG * (k + 1), :], mrow_stacked)

                def store(at):
                    sp.wait_ge(d_done, RING_D.count(at, ("out", 1)))
                    load(rows_of(x1_dram, at[1]), res[:, :, :], x1_stored)

                def load_residual(b):
                    load(res[:, :, :], rows_of(x, b), residual_loaded)

                load_residual(0)
                sp.wait_ge(parts_done, 1)
                stack(0, "q")
                sp.wait_ge(parts_done, 2)
                stack(0, "k")
                stack(1)
                sp.wait_ge(parts_done, 3)
                stack(2)
                max_rows(("before", 0), 0)
                stack(3)
                sp.wait_ge(bias_split, 1)
                sp.wait_ge(pool_setup, 3)
                for k in range(PARTS):
                    load(mk[SK + k:SK + k + 1, :, :], b1p[k], bias_rows)
                    load(b2s[LEAVES * k:LEAVES * (k + 1), :, :], b2p[k][LEAVES * k:LEAVES * (k + 1)], bias_rows)
                with sp.Fori(0, B - 1) as b:
                    at = ("batch", b)
                    sp.wait_ge(xn_done, b + 1)
                    load(x_in, rows_of(x, b + 1), x_loaded)
                    sp.wait_ge(pv_done, UNITS * b + 1)
                    load(ctx_in[:, :, :], rows_of(ctx, b + 1), ctx_loaded)
                    max_rows(at, 1)
                    max_rows(at, 2)
                    sp.wait_ge(parts_done, 3 * b + 5)
                    stack(0)
                    sp.wait_ge(pv_done, UNITS * b + 2 * JT)
                    stack(1)
                    max_rows(at, 3)
                    sp.wait_ge(pv_done, UNITS * b + 3 * JT)
                    stack(2)
                    max_rows(at, 0)
                    sp.wait_ge(pv_done, UNITS * b + 4 * JT)
                    stack(3)
                    store(at)
                    sp.wait_ge(x1_stored, 16 * (b + 1))
                    load_residual(b + 1)
                at = ("last", B - 1)
                for g in range(1, G):
                    max_rows(at, g)
                for g in range(G):
                    sp.wait_ge(stacked[g], 16 * STACK * B)
                sp.wait_ge(pv_done, UNITS * (B - 1) + 1)
                sp.wait_ge(x1_stored, 16 * (B - 1))
                load(x1n, rows_of(x1_dram, 0), x1_loaded)
                load_w1(sp, raw2[0], 1, raw2_loaded)
                load_w2(sp, raw2[1], 1, raw2_loaded)
                load_w1(sp, raw2[2], 2, raw2_loaded)
                store(at)
                sp.wait_ge(x1_stored, 16 * B)

            @block.gpsimd
            def _(pool):
                for n, (dst, value) in enumerate(((noderaw, 0.0), (nb[:, :], 0.0))):
                    pool.memset(dst, value).then_inc(raw_zeroed, 1)
                    pool.wait_ge(raw_zeroed, n + 1)
                for n, (dst, value) in enumerate((
                        (half[:, :], -0.5), (mk[SK:P, :, :], 0.0), (ohm[SK:P, :, :], 0.0), (ohm[SK:SK + 1, :, :], 1.0),
                        (gates[SK:P, :], 1.0), (v_sb[:, :, :, DH:VW], 1.0))):
                    pool.memset(dst, value).then_inc(pool_setup, 1)
                    pool.wait_ge(pool_setup, n + 1)
                    if n == 0:
                        pool.wait_ge(var1, 1)
                        pool.tensor_tensor(rstd[:, :], ve[:, :], half[:, :], ALU.pow).then_inc(rstd1_done, 1)
                        pool.wait_ge(rstd1_done, 1)

                def rstd_1(b):
                    pool.wait_ge(var1, b + 1)
                    pool.tensor_tensor(rstd[:, :], ve[:, :], half[:, :], ALU.pow).then_inc(rstd1_done, 1)

                def residual(b):
                    pool.wait_ge(residual_loaded, 16 * (b + 1))
                    for t in range(T):
                        last = pool.tensor_tensor(res[:, t, :], res[:, t, :], bias[:, :], ALU.add)
                    last.then_inc(res_done, 1)

                def causal(at, u):
                    if u % JT >= T:
                        pool.wait_ge(a_done, RING_A.count(at, ("e", u, HG - 1)))
                        pool.tensor_tensor(carrier_p[:, u:u + 1], half[:, 0:1], half[:, 0:1], ALU.add)
                        c = first_column(u % JT)
                        tile = probs[:, u % 3, :, c:c + P]
                        pool.affine_select(tile, tile, [[0, HG], [1, P]], ALU.is_ge, 0.0, base=0,
                                           channel_multiplier=-1).then_inc(masked, 1)

                def third_part(b, n):
                    pool.wait_ge(part2_done, 3 * b + n + 1)
                    pool.tensor_tensor(parts[:, 2, n, :], rest[:, :], parts[:, 1, n, :],
                                       ALU.subtract).then_inc(parts_done, 1)

                for n in range(3):
                    third_part(0, n)
                pool.wait_ge(parts_done, 3)
                pool.memset(ks[SK:SK + 2, :, :], 1.0).then_inc(ones_set, 1)
                pool.wait_ge(ones_set, 1)
                pool.wait_ge(const_loaded, 16 * 4)
                with pool.Fori(0, B - 1) as b:
                    for u in range(UNITS):
                        causal(("batch", b), u)
                        if u in THIRD_AT:
                            third_part(b + 1, THIRD_AT.index(u))
                        if u == STATS_AT:
                            rstd_1(b + 1)
                        if u == 2 * JT + 1:
                            residual(b)
                for u in range(UNITS):
                    causal(("last", B - 1), u)
                    if u == 2 * JT + 1:
                        residual(B - 1)
                    if u == UNITS - 1:
                        pool.wait_ge(var2, 1)
                        pool.tensor_tensor(rstd[:, :], ve[:, :], half[:, :], ALU.pow).then_inc(rstd2_done, 1)

            @block.scalar
            def _(act):
                def high(at, key, dst, signal):
                    act.wait_ge(d_full, RING_D.count(at, key))
                    act.activation(dst, d_slot(at, key), ACT.Copy).then_inc(signal, 1)

                def weight_high(n):
                    raw, split, loaded = weights[n]
                    act.wait_ge(loaded, 32 if loaded is w1q_loaded else 16)
                    act.activation(flat(split[:, 0, :, :]), raw, ACT.Copy).then_inc(w_high, 1)

                def exps(at, u):
                    own, u, later = at, u % UNITS, u // UNITS
                    c = first_column(u % JT)
                    for h in range(HG):
                        act.wait_ge(a_full, RING_A.count(own, ("e", u, h)))
                        if h == 0 and (u >= 3 or later):
                            act.wait_ge(pv_done, UNITS * (at[1] + later) + (u - 2 if u >= 3 else -1))
                        act.activation(probs[:, u % 3, h, c:N], a_slot(own, ("e", u, h))[:, c:N], ACT.Exp,
                                       scale=SCALE1).then_inc(a_done, 1)

                def max_row(at, g, sent):
                    act.wait_ge(a_full, RING_A.count(at, ("m", g)))
                    if sent is not None:
                        act.wait_ge(mrow_stacked, 32 * sent)
                    act.activation(mrow[:, :], a_slot(at, ("m", g))[0:2 * HG, 0:N // 2].bitcast(BF16),
                                   ACT.Copy).then_inc(a_done, 1)

                def front(at, key):
                    if key == ("xT",):
                        high(at, key, flat(xnT[:, 0, :, :]), x_high)
                    elif key == ("cT",):
                        high(at, key, flat(cT[:, 0, :, :]), c_high)
                    else:
                        high(at, key, parts[:, 0, FRONT.index(key) - 2, :], part1_done)

                def values(at, n):
                    act.wait_ge(a_full, RING_A.count(at, ("v", n)))
                    first, count = V_TILES[n][0], len(V_TILES[n])
                    src = a_slot(at, ("v", n))[:, 0:D * count].rearrange("p (t h c) -> p t h c", t=count, h=H)
                    act.activation(v_sb[:, first:first + count, :, 0:DH], src, ACT.Copy).then_inc(a_done, 1)

                def attention(at, more):
                    b = at[1]
                    for u in range(UNITS):
                        if u + 1 < UNITS or more:
                            exps(at, u + 1)
                        if u % JT == M_AT and (u // JT + 1 < G or more):
                            g = u // JT + 1
                            max_row(at, g % G, G * b + g)
                        if more and u in FRONT_AT:
                            front(at, FRONT_AT[u])
                        if u % JT == JT - 1:
                            g = u // JT
                            act.wait_ge(pv_done, UNITS * b + u + 1)
                            if g > 0:
                                act.wait_ge(d_full, RING_D.count(at, ("oT", g - 1)))
                            act.activation(pv_sb[:, :], ps_o[:, :], ACT.Copy).then_inc(pv_copied, 1)
                    if more:
                        for n in range(4):
                            values(at, n)
                    high(at, ("dT",), flat(oT[:, 0, :, :]), heads_high)
                    if more:
                        for n in range(4, len(V_TILES)):
                            values(at, n)

                at0 = ("before", 0)
                load_square(act, raw_q, wq, wq_loaded)
                load_square(act, raw_kv, wkv, wkv_loaded)
                load_square(act, raw_out, wout, wout_loaded)
                load_w1(act, raw_ffn, 0, w1q_loaded)
                weight_high(0)
                weight_high(1)
                for key in FRONT:
                    front(at0, key)
                for n in range(len(V_TILES)):
                    values(at0, n)
                act.wait_ge(node_turned, 1)
                act.activation(node[:, 0, :, :].rearrange("p k n -> p (k n)"), ps_o[:, 0:KC * 96],
                               ACT.Copy).then_inc(node_high, 1)
                weight_high(2)
                weight_high(3)
                act.wait_ge(w_split, 4)
                load_w2(act, raw_ffn, 0, w2q_loaded)
                weight_high(4)
                max_row(at0, 0, None)
                for h in range(HG):
                    act.wait_ge(a_full, RING_A.count(at0, ("e", 0, h)))
                    act.activation(probs[:, 0, h, :], a_slot(at0, ("e", 0, h)), ACT.Exp,
                                   scale=SCALE1).then_inc(a_done, 1)
                with act.Fori(0, B - 1) as b:
                    attention(("batch", b), True)
                attention(("last", B - 1), False)

            @block.vector
            def _(dve):
                def link(at, key, ins):
                    ins.then_inc(chain, 1)
                    dve.wait_ge(chain, CHAIN.count(at, key))

                def take(at, key):
                    dve.wait_ge(d_full, RING_D.count(at, key))
                    return d_slot(at, key)

                def done(at, key):
                    dve.wait_ge(d_done, RING_D.count(at, key))

                def weight_low(n):
                    raw, split, loaded = weights[n]
                    dve.wait_ge(w_high, n + 1)
                    low_part(dve, flat(split[:, 1, :, :]), raw, flat(split[:, 0, :, :])).then_inc(w_split, 1)

                def stats_1(at, b):
                    dve.wait_ge(x_loaded, 16 * (b + 1))
                    statistics(dve, x_in, ve, var1, at, link)

                def normalise_1(b):
                    dve.wait_ge(rstd1_done, b + 1)
                    normalise(dve, x_in, xn, xn_done)

                def row_max(at, tile):
                    later, n = tile
                    h, t = n // T, n % T
                    s = take(at, ("s", later, n))
                    dve.tensor_reduce(rowmax[:, h // HG, t, h % HG:h % HG + 1], s[:, 0:N + P * (t + 1)], AX.X,
                                      ALU.max, negate=True).then_inc(d_done, 1)
                    if n % (HG * T) == HG * T - 1:
                        g = h // HG
                        done(at, ("s", later, n))
                        link(at, ("mx", later, g), dve.tensor_copy(mx2[:, g, :, 0, :], rowmax[:, g, :, :]))
                        dve.tensor_tensor(mx2[:, g, :, 1, :], rowmax[:, g, :, :], mx2[:, g, :, 0, :],
                                          ALU.subtract).then_inc(max_split, 1)

                def normalise_heads(at, g):
                    s = take(at, ("oT", g))[:, 0:N].rearrange("p (t h c) -> p t h c", t=T, h=HG)
                    link(at, ("oT", g), dve.reciprocal(rinv[:, g, :, :], s[:, :, :, DH]))
                    dst = o_sb[:, :, HG * DH * g:HG * DH * (g + 1)].rearrange("p t (h c) -> p t h c", h=HG)
                    dve.tensor_tensor(dst, s[:, :, :, 0:DH],
                                      rinv[:, g, :, :].unsqueeze(3).broadcast_to([P, T, HG, DH]),
                                      ALU.mult).then_inc(d_done, 1)

                def low(at, key, split, signal, value):
                    s = take(at, key)
                    dve.wait_ge(signal, value)
                    low_part(dve, flat(split[:, 1, :, :]), s, flat(split[:, 0, :, :])).then_inc(d_done, 1)

                def front(at, key, b):
                    if key == ("xT",):
                        low(at, key, xnT, x_high, b + 1)
                    elif key == ("cT",):
                        low(at, key, cT, c_high, b + 1)
                    else:
                        s, n = take(at, key), FRONT.index(key) - 2
                        dve.wait_ge(part1_done, 3 * b + n + 1)
                        if n > 0:
                            dve.wait_ge(parts_done, 3 * b + n)
                        dve.tensor_tensor(rest[:, :], s, parts[:, 0, n, :], ALU.subtract).then_inc(d_done, 1)
                        done(at, key)
                        dve.tensor_copy(parts[:, 1, n, :], rest[:, :]).then_inc(part2_done, 1)

                def attention(at, more):
                    b = at[1]
                    for u in range(UNITS):
                        here = unit_tiles(u, more)
                        for tile in here[:1]:
                            row_max(at, tile)
                        if u % JT == 1 and u > JT:
                            normalise_heads(at, u // JT - 1)
                        for tile in here[1:]:
                            row_max(at, tile)
                        if more and u in FRONT_AT:
                            front(at, FRONT_AT[u], b + 1)
                        if more and u == STATS_AT:
                            stats_1(at, b + 1)
                        if more and u == NORM_AT:
                            normalise_1(b + 1)
                        if not more and u == 3 * JT + 1:
                            dve.wait_ge(x1_loaded, 16)
                            statistics(dve, x1n, ve, var2, at, link, "ln2")
                    normalise_heads(at, G - 1)
                    if more:
                        row_max(at, tail_tile(0))
                        row_max(at, tail_tile(1))
                    low(at, ("dT",), oT, heads_high, b + 1)
                    if more:
                        row_max(at, tail_tile(2))
                        row_max(at, tail_tile(3))
                    else:
                        dve.wait_ge(rstd2_done, 1)
                        normalise(dve, x1n, x1n, yn_done)
                    dve.wait_ge(res_done, b + 1)
                    for c in range(2):
                        s = take(at, ("out", c)).rearrange("p (t d) -> p t d", d=D)[:, 0:2, :]
                        rows = res[:, 2 * c:2 * c + 2, :]
                        dve.tensor_tensor(rows, rows, s, ALU.add).then_inc(d_done, 1)

                at0 = ("before", 0)
                dve.memset(ps_o[:, :], 0.0).then_inc(dve_setup, 1)
                stats_1(at0, 0)
                normalise_1(0)
                weight_low(0)
                weight_low(1)
                front(at0, ("cT",), 0)
                front(at0, ("xT",), 0)
                dve.wait_ge(const_loaded, 16 * 4)
                dve.tensor_scalar(mk[0:SK, :, :].rearrange("p t (a c) -> p (t a) c", a=2),
                                  path[:, :].unsqueeze(2).broadcast_to([SK, BR * LEAVES, LEAF_W]), BIG, None,
                                  ALU.mult).then_inc(dve_setup, 1)
                for k in range(PARTS):
                    last = dve.tensor_copy(ohm[0:SK, :, LEAVES * k:LEAVES * (k + 1)],
                                           path[:, :].rearrange("p (r l) -> p r l", r=BR))
                last.then_inc(dve_setup, 1)
                front(at0, ("q",), 0)
                dve.wait_ge(raw_loaded, 16 * BR * 8)
                for name, raw, rem, p3 in (("b2", b2raw, b2rem, b2p), ("b1", b1raw, b1rem, b1p)):
                    link(at0, (name, 0), dve.tensor_copy(p3[0], raw))
                    link(at0, (name, 1), dve.tensor_tensor(rem, raw, p3[0], ALU.subtract))
                    link(at0, (name, 2), dve.tensor_copy(p3[1], rem))
                    last = dve.tensor_tensor(p3[2], rem, p3[1], ALU.subtract)
                    if name == "b2":
                        link(at0, (name, 3), last)
                last.then_inc(bias_split, 1)
                front(at0, ("k", 0), 0)
                front(at0, ("k", 1), 0)
                dve.wait_ge(ident_loaded, 16)
                dve.tensor_copy(identb[:, :], identf[:, :]).then_inc(dve_setup, 1)
                dve.tensor_copy(maskb[:, :], maskf).then_inc(dve_setup, 1)
                dve.wait_ge(node_high, 1)
                low_part(dve, node[:, 1, :, :].rearrange("p k n -> p (k n)"), ps_o[:, 0:KC * 96],
                         node[:, 0, :, :].rearrange("p k n -> p (k n)")).then_inc(node_done, 1)
                weight_low(2)
                weight_low(3)
                for n in range(LEAD):
                    row_max(at0, (0, n))
                weight_low(4)
                with dve.Fori(0, B - 1) as b:
                    attention(("batch", b), True)
                attention(("last", B - 1), False)

            @block.tensor
            def _(pe):
                def open_d(at, key, source=None):
                    RING_D.wait_free(pe, at, key, d_done, source)
                    return d_slot(at, key)

                def open_a(at, key):
                    RING_A.wait_free(pe, at, key, a_done)
                    return a_slot(at, key)

                def row_scores(at, tile):
                    later, n = tile
                    h, t = n // T, n % T
                    if n % (HG * T) == 0:
                        pe.wait_ge(stacked[h // HG], 16 * STACK * (at[1] + later + 1))
                    s = open_d(at, ("s", later, n))
                    q = qs[0:SK, h, tiles(t)]
                    pe.matmul(s[:, 0:N], q, ks[0:SK, h, 0:N], start=True, stop=True)
                    c = N + P * t
                    pe.matmul(s[:, N:c + P], q, ks[0:SK, h, N:c + P], start=True, stop=False)
                    pe.matmul(s[:, c:c + P], identb[:, :], maskb[:, :], start=False, stop=True).then_inc(d_full, 1)

                def turn_max(at, g, number):
                    pe.wait_ge(max_split, number)
                    s = open_a(at, ("m", g))[:, 0:N // 2].bitcast(BF16)
                    for t in range(T):
                        mm = pe.transpose(s[0:2 * HG, tiles(t)], mx2[:, g, t, :, :].rearrange("p k h -> p (k h)"),
                                          identb[:, :])
                    mm.then_inc(a_full, 1)

                def key_scores(at, u, heads):
                    if u % JT == 0 and heads[0] == 0:
                        pe.wait_ge(mrow_stacked, 32 * (G * at[1] + u // JT + 1))
                    u = u % UNITS
                    g, jt = u // JT, u % JT
                    c = first_column(jt)
                    for h in heads:
                        s = open_a(at, ("e", u, h))
                        pe.matmul(s[:, c:N], ks[0:SK + 2, HG * g + h, tiles(jt)], qs[0:SK + 2, HG * g + h, c:N],
                                  start=True, stop=True).then_inc(a_full, 1)

                def weigh(at, u):
                    g, jt = u // JT, u % JT
                    c = first_column(jt)
                    b = at[1]
                    if jt == 0 and g > 0:
                        pe.wait_ge(pv_copied, G * b + g)
                    if u == 0:
                        pe.wait_ge(a_done, RING_A.per * b + len(RING_A.number["before"]))
                    elif jt < T:
                        pe.wait_ge(a_done, RING_A.count(at, ("e", u, HG - 1)))
                    else:
                        pe.wait_ge(masked, G * T * b + T * g + jt - T + 1)
                    for h in range(HG):
                        mm = pe.matmul(ps_o[32 * h:32 * h + VW, c:N], v_sb[:, jt, HG * g + h, :],
                                       probs[:, u % 3, h, c:N], start=(jt == 0), stop=(jt == JT - 1))
                    mm.then_inc(pv_done, 1)

                def turn_heads(at, g):
                    pe.wait_ge(pv_copied, G * at[1] + g + 1)
                    s = open_d(at, ("oT", g))
                    for t in range(T):
                        mm = pe.transpose(s[:, tiles(t)], pv_sb[:, tiles(t)], identf[:, :])
                    mm.then_inc(d_full, 1)

                def front(at, key, b):
                    if key == ("xT",):
                        pe.wait_ge(xn_done, b + 1)
                        mm = turn_rows(pe, open_d(at, key), xn)
                    elif key == ("cT",):
                        pe.wait_ge(ctx_loaded, 16 * (b + 1))
                        mm = turn_rows(pe, open_d(at, key), ctx_in)
                    elif key == ("q",):
                        if at[0] != "before":
                            pe.wait_ge(stacked[G - 1], 16 * STACK * b)
                        s = open_d(at, key, ("xT",))
                        for f in range(2):
                            mm = product(pe, s[:, N * f:N * (f + 1)],
                                         [(both(wq_sb, k, tiles(f)), both(xnT, k, slice(0, N))) for k in range(KC)])
                    else:
                        s, f = open_d(at, key, ("cT",)), key[1]
                        for c, src in enumerate((cT, xnT)):
                            mm = product(pe, s[:, N * c:N * (c + 1)],
                                         [(both(wkv_sb, k, tiles(f)), both(src, k, slice(0, N))) for k in range(KC)])
                    mm.then_inc(d_full, 1)

                def values(at, n):
                    s = open_a(at, ("v", n))
                    for i, tile in enumerate(V_TILES[n]):
                        src = (cT, xnT)[tile // T]
                        mm = product(pe, s[:, D * i:D * (i + 1)],
                                     [(both(src, k, tiles(tile % T)), both(wkv_sb, k, slice(D, 2 * D)))
                                      for k in range(KC)])
                    mm.then_inc(a_full, 1)

                def attention(at, more):
                    b = at[1]
                    for u in range(UNITS):
                        tiles_here = unit_tiles(u, more)
                        for k in range(2):
                            if k == 1 and u - 1 in FRONT_AT:
                                weigh(at, u)
                            if u + 1 < UNITS or more:
                                key_scores(at, u + 1, (2 * k, 2 * k + 1))
                            if k == 1 and u % JT == 1 and u > JT and u - 1 in FRONT_AT:
                                turn_heads(at, u // JT - 1)
                            for tile in tiles_here[:1] if k == 0 else tiles_here[1:]:
                                row_scores(at, tile)
                            if k == 0 and u % JT == 1 and u > JT and u - 1 not in FRONT_AT:
                                turn_heads(at, u // JT - 1)
                        if u % JT == M_AT and (u // JT + 1 < G or more):
                            g = u // JT + 1
                            turn_max(at, g % G, G * b + g + 1)
                        if u - 1 not in FRONT_AT:
                            weigh(at, u)
                        if more and u in FRONT_AT:
                            front(at, FRONT_AT[u], b + 1)
                    if more:
                        values(at, 0)
                        values(at, 1)
                    turn_heads(at, G - 1)
                    if more:
                        for n in range(2):
                            values(at, 2 + n)
                            row_scores(at, tail_tile(n))
                    turn_rows(pe, open_d(at, ("dT",), ("oT", G - 1)), o_sb).then_inc(d_full, 1)
                    if more:
                        for n in range(2, 4):
                            values(at, 2 + n)
                            row_scores(at, tail_tile(n))
                    for c in range(2):
                        s = open_d(at, ("out", c), ("dT",))
                        for k2 in range(2):
                            mm = product(pe, s[:, D * k2:D * (k2 + 1)],
                                         [(both(oT, k, tiles(2 * c + k2)), both(wout_sb, k, slice(0, D)))
                                          for k in range(KC)])
                        mm.then_inc(d_full, 1)

                at0 = ("before", 0)
                pe.wait_ge(ident_loaded, 16)
                front(at0, ("cT",), 0)
                front(at0, ("xT",), 0)
                pe.wait_ge(w_split, 1)
                front(at0, ("q",), 0)
                pe.wait_ge(w_split, 2)
                front(at0, ("k", 0), 0)
                front(at0, ("k", 1), 0)
                for n in range(len(V_TILES)):
                    values(at0, n)
                pe.wait_ge(raw_loaded, 16 * BR * 8)
                pe.wait_ge(dve_setup, 1)
                for k in range(KC):
                    mm = pe.transpose(ps_o[:, 96 * k:96 * (k + 1)], noderaw[:, tiles(k)], identf[0:96, 0:96])
                mm.then_inc(node_turned, 1)
                pe.wait_ge(pool_setup, 6)
                pe.wait_ge(dve_setup, 5)
                for n in range(LEAD):
                    row_scores(at0, (0, n))
                    if n == HG * T + 1:
                        turn_max(at0, 0, 1)
                pe.wait_ge(ones_set, 1)
                pe.wait_ge(w_split, 5)
                pe.wait_ge(mrow_stacked, 32)
                for h in range(HG):
                    s = open_a(at0, ("e", 0, h))
                    pe.matmul(s, ks[0:SK + 2, h, tiles(0)], qs[0:SK + 2, h, :],
                              start=True, stop=True).then_inc(a_full, 1)
                pe.wait_ge(node_done, 1)
                pe.wait_ge(bias_rows, 16 * 2 * PARTS)
                with pe.Fori(0, B - 1) as b:
                    attention(("batch", b), True)
                attention(("last", B - 1), False)

        with ExitStack() as es:
            def sb2(name, shape, dt=F32):
                return es.enter_context(nc.sbuf_tensor(name, shape, dt))

            p2 = work[:, 0:2048].rearrange("p (t n) -> p t n", t=T)
            res = work[:, 2048:3072].rearrange("p (t d) -> p t d", t=T)
            w1 = [w1q] + [sb2(f"w1{r}", [P, 2, KC, HID], F32R) for r in "kv"]
            w2 = [w2q] + [sb2(f"w2{r}", [P, 2, HT, D], F32R) for r in "kv"]
            splits = [w1[1], w2[1], w1[2], w2[2]]
            yT = sb2("yT", [P, 2, KC, N], F32R)
            hidden = sb2("hidden", [P, 2, HT, N], F32R)
            p2T = hidden
            qk2T = [sb2(f"{r}2T", [P, 2, KC, N], F32R) for r in "qk"]
            v2 = sb2("v2", [P, 2, T, D], F32R)
            onehot = sb2("onehot", [48, BR, N], BF16)
            g0 = sb2("g0", [96, N], BF16)
            nmax, nmaxs = sb2("nmax", [P, T]), sb2("nmaxs", [P, T])
            sums, rs2 = sb2("sums", [P, T]), sb2("rs2", [P, T])

            def h_slot(at, key):
                return ps_a[:, RING_H.slot(at, key), :]

            def f_slot(at, key):
                return ps_d[:, RING_F.slot(at, key), :]

            block = es.enter_context(nc.Block())

            @block.sync
            def _(sp):
                def load(dst, src, signal):
                    sp.dma_start(dst, src).then_inc(signal, 16)

                sp.wait_ge(w2_split, 1)
                load(raw2[3].rearrange("p (t d) -> p t d", t=HT),
                     ffn[2][4].rearrange("(t a) h d -> (a h) t d", a=2), last_loaded)

                def store(at):
                    sp.wait_ge(f_done, RING_F.count(at, ("y", 1)))
                    load(rows_of(out, at[1]), res, stored)

                sp.wait_ge(w2_split, 2)
                load(res, rows_of(x1_dram, 0), res_loaded)
                with sp.Fori(0, B - 1) as b:
                    sp.wait_ge(h_done, RING_H.per * b + len(RING_H.number["before"]))
                    load(x1n, rows_of(x1_dram, b + 1), x1_loaded)
                    store(("batch", b))
                    sp.wait_ge(stored, 16 * (b + 1))
                    load(res, rows_of(x1_dram, b + 1), res_loaded)
                store(("last", B - 1))
                sp.wait_ge(stored, 16 * B)

            @block.gpsimd
            def _(pool):
                def rstd_2(b):
                    pool.wait_ge(var2, b + 1)
                    pool.tensor_tensor(rstd[:, :], ve[:, :], half[:, :], ALU.pow).then_inc(rstd2_done, 1)

                for n in range(4):
                    if n < 3:
                        pool.wait_ge(w2_high, n + 1)
                    else:
                        pool.wait_ge(last_loaded, 16)
                        pool.tensor_copy(flat(splits[n][:, 0, :, :]), raw2[n]).then_inc(w2_last_high, 1)
                        pool.wait_ge(w2_last_high, 1)
                    pool.tensor_tensor(flat(splits[n][:, 1, :, :]), raw2[n], flat(splits[n][:, 0, :, :]).bitcast(F32),
                                       ALU.subtract).then_inc(w2_split, 1)
                with pool.Fori(0, B - 1) as b:
                    rstd_2(b + 1)

            @block.scalar
            def _(act):
                def high(at, key, dst, func=ACT.Copy):
                    act.wait_ge(h_full, RING_H.count(at, key))
                    act.activation(dst, h_slot(at, key), func).then_inc(h_high, 1)

                def branch_high(at, r, dst):
                    act.wait_ge(f_full, RING_F.count(at, ("f", r)))
                    act.activation(dst, f_slot(at, ("f", r)), ACT.Copy).then_inc(f_high, 1)

                def feedforward(at, more):
                    b = at[1]
                    for r in range(BR):
                        for t in range(HT):
                            high(at, ("h", r, t), hidden[:, 0, t, :], ACT.Relu)
                        if r < 2:
                            branch_high(at, r, flat(qk2T[r][:, 0, :, :]))
                    if more:
                        for k in range(KC):
                            high(at, ("yT", k), yT[:, 0, k, :])
                    for t in range(T):
                        act.wait_ge(x_max, T * b + t + 1)
                        act.activation(p2[:, t, :], ps_o[:, :], ACT.Exp, bias=nmaxs[:, t:t + 1], scale=SCALE2,
                                       accum_out=sums[:, t:t + 1]).then_inc(x_done, 1)
                    branch_high(at, 2, flat(v2[:, 0, :, :]))
                    for t in range(T):
                        high(at, ("pT", t), p2T[:, 0, t, :])

                for k in range(KC):
                    high(("before", 0), ("yT", k), yT[:, 0, k, :])
                act.wait_ge(raw2_loaded, 16 * 5)
                for n in range(3):
                    act.activation(flat(splits[n][:, 0, :, :]), raw2[n], ACT.Copy).then_inc(w2_high, 1)
                with act.Fori(0, B - 1) as b:
                    feedforward(("batch", b), True)
                feedforward(("last", B - 1), False)

            @block.vector
            def _(dve):
                def link(at, key, ins):
                    ins.then_inc(chain2, 1)
                    dve.wait_ge(chain2, CHAIN2.count(at, key))

                def take(at, key):
                    dve.wait_ge(f_full, RING_F.count(at, key))
                    return f_slot(at, key)

                def low(at, key, dst, high):
                    dve.wait_ge(h_high, HIGH_H.count(at, key))
                    low_part(dve, dst, h_slot(at, key), high).then_inc(h_done, 1)

                def branch_low(at, r, split):
                    dve.wait_ge(f_high, BR * at[1] + r + 1)
                    low_part(dve, flat(split[:, 1, :, :]), f_slot(at, ("f", r)),
                             flat(split[:, 0, :, :])).then_inc(f_done, 1)

                def stats_2(at, b):
                    dve.wait_ge(x1_loaded, 16 * (b + 1))
                    statistics(dve, x1n, ve, var2, at, link)

                def normalise_2(b):
                    dve.wait_ge(rstd2_done, b + 1)
                    normalise(dve, x1n, x1n, yn_done)

                def decisions(at, b):
                    s = take(at, ("node",))
                    dve.tensor_scalar(g0[:, :], s[0:96, 0:N], nb[:, 0:1], 0.0, ALU.add, ALU.is_ge).then_inc(f_done, 1)
                    dve.wait_ge(f_done, RING_F.count(at, ("node",)))
                    dve.tensor_scalar(gates[0:96, :], g0[:, :], flip[:, 0:1], None,
                                      ALU.not_equal).then_inc(gates_done, 1)

                def chosen_leaves(at):
                    for r in range(BR):
                        dve.wait_ge(h_full, RING_H.count(at, ("one", r)))
                        dve.tensor_scalar(onehot[:, r, :], h_slot(at, ("one", r))[0:48], 0.0, None,
                                          ALU.max).then_inc(h_done, 1)

                def feedforward(at, more):
                    b = at[1]
                    for r in range(BR):
                        for t in range(HT):
                            key = ("h", r, t)
                            dve.wait_ge(h_high, HIGH_H.count(at, key))
                            dve.scalar_tensor_tensor(out=hidden[:, 1, t, :], in0=h_slot(at, key), scalar=0.0,
                                                     in1=hidden[:, 0, t, :].bitcast(F32), op0=ALU.max,
                                                     op1=ALU.subtract).then_inc(h_done, 1)
                        if r == 1 and more:
                            stats_2(at, b + 1)
                            normalise_2(b + 1)
                        if r < 2:
                            branch_low(at, r, qk2T[r])
                    if more:
                        for k in range(KC):
                            low(at, ("yT", k), yT[:, 1, k, :], yT[:, 0, k, :])
                    for t in range(T):
                        dve.wait_ge(x_full, T * b + t + 1)
                        link(at, ("x", t), dve.tensor_reduce(nmax[:, t:t + 1], ps_o[:, :], AX.X, ALU.max,
                                                             negate=True))
                        dve.tensor_scalar(nmaxs[:, t:t + 1], nmax[:, t:t + 1], SCALE2, None,
                                          ALU.mult).then_inc(x_max, 1)
                    branch_low(at, 2, v2)
                    for t in range(T):
                        if t == 2 and more:
                            decisions(at, b + 1)
                        low(at, ("pT", t), p2T[:, 1, t, :], p2T[:, 0, t, :])
                    dve.wait_ge(x_done, T * b + T)
                    link(at, ("sum",), dve.reciprocal(rs2[:, :], sums[:, :]))
                    dve.wait_ge(res_loaded, 16 * (b + 1))
                    for c in range(2):
                        s = take(at, ("y", c)).rearrange("p (t d) -> p t d", d=D)
                        for k in range(2):
                            t = 2 * c + k
                            last = dve.scalar_tensor_tensor(out=res[:, t, :], in0=s[:, k, :],
                                                            scalar=rs2[:, t:t + 1], in1=res[:, t, :],
                                                            op0=ALU.mult, op1=ALU.add)
                        last.then_inc(f_done, 1)
                        if c == 0 and more:
                            chosen_leaves(at)

                at0 = ("before", 0)
                for k in range(KC):
                    low(at0, ("yT", k), yT[:, 1, k, :], yT[:, 0, k, :])
                decisions(at0, 0)
                chosen_leaves(at0)
                with dve.Fori(0, B - 1) as b:
                    feedforward(("batch", b), True)
                feedforward(("last", B - 1), False)

            @block.tensor
            def _(pe):
                def open_f(at, key, source=None):
                    RING_F.wait_free(pe, at, key, f_done, source)
                    return f_slot(at, key)

                def open_h(at, key):
                    RING_H.wait_free(pe, at, key, h_done)
                    return h_slot(at, key)

                def turned(at, b):
                    pe.wait_ge(yn_done, b + 1)
                    for k in range(KC):
                        s = open_h(at, ("yT", k))
                        for t in range(T):
                            mm = pe.transpose(s[:, tiles(t)], x1n[:, t, tiles(k)], identf[:, :])
                        mm.then_inc(h_full, 1)

                def decide(at):
                    pe.wait_ge(h_done, RING_H.count(at, TURN_Y[-1]))
                    s = open_f(at, ("node",))
                    product(pe, s[0:96, 0:N], [(both(node, k, slice(0, 96)), both(yT, k, slice(0, N)))
                                               for k in range(KC)]).then_inc(f_full, 1)

                def choose_leaves(at, b):
                    pe.wait_ge(gates_done, b + 1)
                    for r in range(BR):
                        s = open_h(at, ("one", r))
                        pe.matmul(s[0:48, :], ohm[:, r, :], gates[:, :], start=True, stop=True).then_inc(h_full, 1)

                def hidden_layer(at, r):
                    for t in range(HT):
                        s = open_h(at, ("h", r, t))
                        product(pe, s, [(both(w1[r], k, tiles(t)), both(yT, k, slice(0, N))) for k in range(KC)],
                                last=False)
                        pe.matmul(s, mk[:, HT * r + t, :], gates[:, :], start=False, stop=True).then_inc(h_full, 1)

                def feedforward(at, more):
                    b = at[1]
                    for r in range(2):
                        if r > 0:
                            pe.wait_ge(w2_split, 2)
                        hidden_layer(at, r)
                        s = open_f(at, ("f", r))
                        for t in range(HT):
                            pe.wait_ge(h_done, RING_H.count(at, ("h", r, t)))
                            for k in range(KC):
                                product(pe, s[:, N * k:N * (k + 1)],
                                        [(both(w2[r], t, tiles(k)), both(hidden, t, slice(0, N)))],
                                        first=(t == 0), last=False)
                        for k in range(KC):
                            mm = pe.matmul(s[:, N * k:N * (k + 1)], b2s[:, r, tiles(k)], onehot[:, r, :],
                                           start=False, stop=True)
                        mm.then_inc(f_full, 1)
                    pe.wait_ge(w2_split, 4)
                    hidden_layer(at, 2)
                    if more:
                        turned(at, b + 1)
                    pe.wait_ge(f_done, RING_F.count(at, ("f", 1)))
                    for t in range(T):
                        if t > 0:
                            pe.wait_ge(x_done, T * b + t)
                        product(pe, ps_o[:, :], [(both(qk2T[0], k, tiles(t)), both(qk2T[1], k, slice(0, N)))
                                                 for k in range(KC)]).then_inc(x_full, 1)
                        if t == 0:
                            v = open_f(at, ("f", 2))
                            pe.wait_ge(h_done, RING_H.count(at, ("h", 2, HT - 1)))
                        s = v[:, D * t:D * (t + 1)]
                        product(pe, s, [(both(hidden, j, tiles(t)), both(w2[2], j, slice(0, D))) for j in range(HT)],
                                last=False)
                        mm = pe.matmul(s, onehot[:, 2, tiles(t)], b2s[:, 2, :], start=False, stop=True)
                    mm.then_inc(f_full, 1)
                    for t in range(T):
                        if t == T - 1 and more:
                            decide(at)
                        s = open_h(at, ("pT", t))
                        pe.wait_ge(x_done, T * b + t + 1)
                        for j in range(T):
                            mm = pe.transpose(s[:, tiles(j)], p2[:, t, tiles(j)], identf[:, :])
                        mm.then_inc(h_full, 1)
                    pe.wait_ge(f_done, RING_F.count(at, ("f", 2)))
                    for c in range(2):
                        s = open_f(at, ("y", c))
                        for k in range(2):
                            t = 2 * c + k
                            pe.wait_ge(h_done, RING_H.count(at, ("pT", t)))
                            mm = product(pe, s[:, D * k:D * (k + 1)],
                                         [(both(p2T, t, tiles(j)), both(v2, j, slice(0, D))) for j in range(T)])
                        mm.then_inc(f_full, 1)
                        if c == 0 and more:
                            choose_leaves(at, b + 1)

                at0 = ("before", 0)
                turned(at0, 0)
                decide(at0)
                choose_leaves(at0, 0)
                with pe.Fori(0, B - 1) as b:
                    feedforward(("batch", b), True)
                feedforward(("last", B - 1), False)


def constants():
    import numpy as np

    ident = np.eye(P, dtype=np.float32)
    mask = np.where(np.arange(P)[None, :] > np.arange(P)[:, None], np.float32(-BIG), np.float32(0))
    path = np.zeros((96, BR * LEAVES), np.float32)
    flip = np.zeros((96, 1), np.float32)
    for r in range(BR):
        flip[32 * r + NODES:32 * r + 2 * NODES] = 1
        for leaf in range(LEAVES):
            node = leaf + NODES
            while node:
                right, node = (node - 1) % 2, (node - 1) // 2
                path[32 * r + node + (NODES if right else 0), r * LEAVES + leaf] = -1
    return {"c_ident": ident, "c_mask": mask.astype(np.float32), "c_path": path, "c_flip": flip}


_FFN = ["node_w", "node_b", "w1", "b1", "w2", "b2"]
_INS = (["x", "ctx_1024", "L0_xattn_Wq", "L0_xattn_Wkv", "L0_xattn_Wout", "L0_xattn_bout"]
        + [f"L0_ffn_{r}_{n}" for r in "qkv" for n in _FFN])


def by_column(w):
    return w.reshape(D, G, HG, DH).transpose(0, 1, 3, 2).reshape(D, D)


def kernel(**inputs):
    import numpy as _np
    import concourse.bacc as _bacc
    from concourse import mybir as _mybir
    from concourse.bass_utils import run_bass_kernel_spmd as _run

    nc = _bacc.Bacc("TRN2", target_bir_lowering=False, num_devices=1)
    arrays, args = {}, []
    consts = constants()
    for name in _INS + list(consts):
        a = _np.asarray(inputs[name] if name in inputs else consts[name])
        if name == "L0_xattn_Wq":
            a = by_column(a)
        if name == "L0_xattn_Wkv":
            a = _np.concatenate([by_column(a[:, :D]), a[:, D:]], axis=1)
        a = _np.ascontiguousarray(a)
        arrays[f"in_{name}_dram"] = a
        args.append(nc.dram_tensor(f"in_{name}_dram", a.shape, _mybir.dt.from_np(a.dtype), kind="ExternalInput").ap())
    out = nc.dram_tensor("out_0_dram", (B, N, D), _mybir.dt.float32, kind="ExternalOutput").ap()
    ffn = [args[6 + 6 * r:12 + 6 * r] for r in range(BR)]
    program(nc, *args[:6], ffn, *args[24:28], out)
    r = _run(nc, [arrays], core_ids=[0])
    return r.results[0]["out_0_dram"]
```
